# Optimizing a Trainium2 kernel written in Bass

```python
import numpy as np
import jax
import jax.numpy as jnp

def _softmax(x, axis=-1):
    return jax.nn.softmax(x, axis=axis)

def _gelu(x):
    return jax.nn.gelu(x, approximate=True)

def _silu(x):
    return jax.nn.silu(x)

def _sigmoid(x):
    return jax.nn.sigmoid(x)

def _layernorm(x, axis=-1, eps=1e-05):
    m = jnp.mean(x, axis=axis, keepdims=True)
    v = jnp.var(x, axis=axis, keepdims=True)
    return (x - m) / jnp.sqrt(v + eps)

def _scatter_add(tgt, idx, src, axis=0):
    return tgt.at[idx].add(src)

def _segment_sum(src, seg, n):
    return jax.ops.segment_sum(src, seg, n)
kernel_name = 'mk_xattn_ffn_d1_seqx_r8_e438d3'

def setup_inputs(seed: int=0):
    np.random.seed(seed)
    _w = jnp.asarray

    def _rec_inputs():
        import jax
        import jax.numpy as jnp
        _rk = jax.random.key(seed)
        x = 7.22e-05 + 1 * jax.random.normal(jax.random.fold_in(_rk, 1), (64, 64, 128), jnp.float32)
        _lenS = 64 - jax.random.randint(jax.random.fold_in(_rk, 7), (64,), 0, max(1, 64 // 4) + 1, jnp.int32)
        _lenS2 = 64 - jax.random.randint(jax.random.fold_in(_rk, 8), (64,), 0, max(1, 64 // 4) + 1, jnp.int32)
        _ctx_1024P = jax.random.normal(jax.random.fold_in(_rk, 11), (64, 16, 128), jnp.float32)
        _ctx_1024c = jax.random.dirichlet(jax.random.fold_in(_rk, 511), 0.3 * jnp.ones((16,), jnp.float32), (64, 64))
        _ctx_1024t = jnp.einsum('bsk,bkd->bsd', _ctx_1024c, _ctx_1024P)
        _ctx_1024t = _ctx_1024t * jax.lax.rsqrt(jnp.mean(jnp.square(_ctx_1024t)) + 1e-12) * 0.953939
        ctx_1024 = 4.13588e-05 + 0.999923 * (_ctx_1024t + 0.3 * jax.random.normal(jax.random.fold_in(_rk, 611), (64, 64, 128), jnp.float32))
        _validS = jnp.arange(64)[None, :] < _lenS[:, None]
        _validS2 = jnp.arange(64)[None, :] < _lenS2[:, None]
        _causal = jnp.tril(jnp.ones((64, 64), dtype=bool))
        mask_BxS2_ff1 = jnp.where(jnp.ones((64, 64), dtype=bool), 1.0, 0.0).astype(jnp.float32)
        return (x, ctx_1024, mask_BxS2_ff1)
    x, ctx_1024, mask_BxS2_ff1 = _rec_inputs()

    def _L0_xattn_setup():
        import jax, jax.numpy as jnp
        import numpy as np
        NUM_HEADS = 16
        key = jax.random.key(seed)
        ks = jax.random.split(key, 8)
        B, S, D = (4, 256, 128)
        scale = 1.0 / np.sqrt(D)
        return {'query': jax.random.normal(ks[0], (B, S, D), dtype=jnp.float32), 'key': jax.random.normal(ks[1], (B, S, D), dtype=jnp.float32), 'value': jax.random.normal(ks[2], (B, S, D), dtype=jnp.float32), 'mask': jnp.ones((B, S), dtype=jnp.float32), 'Wq': jax.random.normal(ks[3], (D, D), dtype=jnp.float32) * scale, 'bq': jnp.zeros((D,), dtype=jnp.float32), 'Wk': jax.random.normal(ks[4], (D, D), dtype=jnp.float32) * scale, 'bk': jnp.zeros((D,), dtype=jnp.float32), 'Wv': jax.random.normal(ks[5], (D, D), dtype=jnp.float32) * scale, 'bv': jnp.zeros((D,), dtype=jnp.float32), 'Wo': jax.random.normal(ks[6], (D, D), dtype=jnp.float32) * scale, 'bo': jnp.zeros((D,), dtype=jnp.float32)}
    _L0_xattn_all = _L0_xattn_setup()
    _L0_xattn_in = {k: v for k, v in _L0_xattn_all.items() if k in ('Wq', 'bq', 'Wk', 'bk', 'Wv', 'bv', 'Wo', 'bo')}
    del _L0_xattn_all

    def _L0_ffn_setup():
        import jax, jax.numpy as jnp
        import numpy as np
        N_EXP = 8
        TOP_K = 2
        CAPACITY_FACTOR = 1.25
        key = jax.random.key(seed)
        ks = jax.random.split(key, 5)
        B, T, D = (4, 128, 128)
        H = 4 * D
        E = N_EXP
        x = jax.random.normal(ks[0], (B, T, D), jnp.float32)
        gate_w = jax.random.normal(ks[1], (D, E), jnp.float32) * 0.02
        c_fc = jax.random.normal(ks[2], (E, D, H), jnp.float32) * 0.02
        fc_bias = jnp.zeros((E, 1, H), jnp.float32)
        c_proj = jax.random.normal(ks[3], (E, H, D), jnp.float32) * 0.02
        proj_bias = jnp.zeros((E, 1, D), jnp.float32)
        return dict(x=x, gate_w=gate_w, c_fc=c_fc, fc_bias=fc_bias, c_proj=c_proj, proj_bias=proj_bias)
    _L0_ffn_all = _L0_ffn_setup()
    _L0_ffn_in = {k: v for k, v in _L0_ffn_all.items() if k in ('gate_w', 'c_fc', 'fc_bias', 'c_proj', 'proj_bias')}
    del _L0_ffn_all
    return {'x': x, 'ctx_1024': ctx_1024, 'mask_BxS2_ff1': mask_BxS2_ff1, 'L0_xattn_Wq': _L0_xattn_in['Wq'], 'L0_xattn_bq': _L0_xattn_in['bq'], 'L0_xattn_Wk': _L0_xattn_in['Wk'], 'L0_xattn_bk': _L0_xattn_in['bk'], 'L0_xattn_Wv': _L0_xattn_in['Wv'], 'L0_xattn_bv': _L0_xattn_in['bv'], 'L0_xattn_Wo': _L0_xattn_in['Wo'], 'L0_xattn_bo': _L0_xattn_in['bo'], 'L0_ffn_gate_w': _L0_ffn_in['gate_w'], 'L0_ffn_c_fc': _L0_ffn_in['c_fc'], 'L0_ffn_fc_bias': _L0_ffn_in['fc_bias'], 'L0_ffn_c_proj': _L0_ffn_in['c_proj'], 'L0_ffn_proj_bias': _L0_ffn_in['proj_bias']}

def reference(x, ctx_1024, mask_BxS2_ff1, L0_xattn_Wq, L0_xattn_bq, L0_xattn_Wk, L0_xattn_bk, L0_xattn_Wv, L0_xattn_bv, L0_xattn_Wo, L0_xattn_bo, L0_ffn_gate_w, L0_ffn_c_fc, L0_ffn_fc_bias, L0_ffn_c_proj, L0_ffn_proj_bias):
    import jax
    import jax.numpy as jnp

    def _L0_xattn_ref(query, key, value, mask, Wq, bq, Wk, bk, Wv, bv, Wo, bo):
        import jax, jax.numpy as jnp
        import numpy as np
        NUM_HEADS = 16
        B, S, D = query.shape
        H = NUM_HEADS
        dh = D // H

        def split_heads(x):
            return x.reshape(B, S, H, dh).transpose(0, 2, 1, 3)
        q = split_heads(query @ Wq + bq) * (1.0 / jnp.sqrt(jnp.float32(dh)))
        k = split_heads(key @ Wk + bk)
        v = split_heads(value @ Wv + bv)
        scores = jnp.einsum('bhqd,bhkd->bhqk', q, k)
        m = mask.reshape(B, 1, 1, S).astype(scores.dtype)
        scores = scores - 1e+30 * (1.0 - m)
        weights = jax.nn.softmax(scores, axis=-1)
        context = jnp.einsum('bhqk,bhkd->bhqd', weights, v)
        context = context.transpose(0, 2, 1, 3).reshape(B, S, D)
        return context @ Wo + bo

    def _L0_ffn_ref(x, gate_w, c_fc, fc_bias, c_proj, proj_bias):
        import jax, jax.numpy as jnp
        import numpy as np
        N_EXP = 8
        TOP_K = 2
        CAPACITY_FACTOR = 1.25
        B, T, D = x.shape
        n = B * T
        E, k = (N_EXP, TOP_K)
        cap = int(CAPACITY_FACTOR * n * k / E)
        xt = x.reshape(n, D)
        logits = xt @ gate_w
        top_logits, top_idx = jax.lax.top_k(logits, k)
        masked = jnp.full_like(logits, -jnp.inf)
        masked = masked.at[jnp.arange(n)[:, None], top_idx].set(top_logits)
        router_probs = jax.nn.softmax(masked, axis=-1)
        exp_mask = jax.nn.one_hot(top_idx, E, dtype=jnp.int32)
        exp_mask = jnp.transpose(exp_mask, (1, 0, 2))
        exp_rank = jnp.cumsum(exp_mask.reshape(k * n, E), axis=0) - 1
        exp_rank = exp_rank.reshape(k, n, E)
        exp_mask = exp_mask * (exp_rank < cap).astype(jnp.int32)
        used_capacity = jnp.sum(exp_mask, axis=(0, 1))
        exp_rank = jnp.sum(exp_mask * exp_rank, axis=-1)
        exp_weights = exp_mask.astype(x.dtype) * router_probs[None]
        rank_oh = jax.nn.one_hot(exp_rank, cap, dtype=x.dtype)
        cb_weight = jnp.einsum('kne,knc->nec', exp_weights, rank_oh)
        sec_mask = (cb_weight != 0).astype(x.dtype)
        exp_batches = jnp.einsum('nec,nd->ecd', sec_mask, xt)
        h = jnp.einsum('ecd,edh->ech', exp_batches, c_fc) + fc_bias
        h = jax.nn.gelu(h, approximate=False)
        exp_out = jnp.einsum('ech,ehd->ecd', h, c_proj) + proj_bias
        out = jnp.einsum('nec,ecd->nd', cb_weight, exp_out)
        return out.reshape(B, T, D)
    x = x + _L0_xattn_ref(_layernorm(x, axis=-1), ctx_1024, ctx_1024, mask_BxS2_ff1, L0_xattn_Wq, L0_xattn_bq, L0_xattn_Wk, L0_xattn_bk, L0_xattn_Wv, L0_xattn_bv, L0_xattn_Wo, L0_xattn_bo)
    x = x + _L0_ffn_ref(_layernorm(x, axis=-1), L0_ffn_gate_w, L0_ffn_c_fc, L0_ffn_fc_bias, L0_ffn_c_proj, L0_ffn_proj_bias)
    return x

_drawn_inputs = setup_inputs


def setup_inputs(seed=0):
    import zlib

    import numpy as np

    out = dict(_drawn_inputs(seed))
    spreads = {'L0_xattn_bq': (0.0, 0.298),
     'L0_xattn_bk': (0.0, 0.8),
     'L0_xattn_bv': (0.0, 0.1),
     'L0_xattn_bo': (0.0, 0.1),
     'L0_ffn_fc_bias': (0.0, 0.533),
     'L0_ffn_proj_bias': (0.0, 0.1)}
    factors = {}
    for name, (base, spread) in spreads.items():
        noise = np.random.default_rng([zlib.crc32(name.encode()), seed]).standard_normal(out[name].shape)
        drawn = base * np.exp(spread * noise) if base else spread * noise
        out[name] = jnp.asarray(drawn.astype(out[name].dtype))
    for name, factor in factors.items():
        out[name] = (out[name] * factor).astype(out[name].dtype)
    return out
```

```python
from contextlib import ExitStack

import concourse.bass as bass
import numpy as np
from concourse import mybir

F32 = mybir.dt.float32
BF16 = mybir.dt.bfloat16
I32 = mybir.dt.int32
U32 = mybir.dt.uint32
ALU = mybir.AluOpType
ACT = mybir.ActivationFunctionType
AX = mybir.AxisListType

P = 128
TG = 4
NOWHERE = 1.0e6
EPS = 1e-5


def wait_before(engine, sem, value, met):
    if not isinstance(value, int):
        value = engine.compute_val(value)
    engine.wait_ge(met, 1)
    engine.wait_ge(sem, value)


def wait_later(engine, sem, value):
    if not isinstance(value, int) or value > 0:
        engine.wait_ge(sem, value)


class Chain:

    def __init__(self, engine, sem, per, turn):
        self.engine, self.sem, self.per, self.base, self.k = engine, sem, per, turn * per, 0

    def step(self, instruction):
        self.k += 1
        instruction.then_inc(self.sem, 1)
        self.engine.wait_ge(self.sem, self.base + self.k)

    def mark(self, instruction):
        self.k += 1
        instruction.then_inc(self.sem, 1)

    def end(self):
        assert self.k == self.per, (self.k, self.per)


def xattn_moe(nc, x, ctx_in, mask, wq, bq, wk, bk, wv, bv, wo, bo, gate_w, c_fc, fc_bias, c_proj, proj_bias, out):
    B, S, D = x.shape
    E, _, HID = c_fc.shape
    N = B * S
    H, DH = 16, D // 16
    PAIRS = H // 2
    GROUPS = N // (TG * P)
    TILES = N // P
    BG = TG * P // S
    TOK = TG * P
    CAP = int(1.25 * N * 2 / E)
    J = CAP // P
    HC = HID // P
    LINE = 2 * N
    ROW = D + 3
    SCALE = float(np.float32(1.0) / np.sqrt(np.float32(DH)))
    LOOPS = (GROUPS - 2) // 2
    assert S == 64 and D == P and CAP == J * P and GROUPS % 2 == 0 and E == 8

    x_v = x.rearrange("b s d -> (b s) d").rearrange("(t p) d -> p t d", p=P)
    ctx_v = ctx_in.rearrange("b s d -> (b s) d").rearrange("(t p) d -> p t d", p=P)
    out_v = out.rearrange("b s d -> (b s) d").rearrange("(t p) d -> p t d", p=P)
    lines = nc.dram_tensor("lines", [E * LINE, ROW], F32, kind="Internal").ap()
    table = nc.dram_tensor("table", [2 * N, D], F32, kind="Internal").ap()
    lines_fill = lines.rearrange("(e l) r -> e l r", e=E)[:, N:N + CAP, :].rearrange("e (p j) r -> p e (j r)", p=P)
    table_v = table.rearrange("(k t p) d -> p k t d", k=2, p=P)

    with ExitStack() as stack:
        def sb(name, shape, dt=F32):
            return stack.enter_context(nc.sbuf_tensor(name, shape, dt))

        def sem(name):
            return stack.enter_context(nc.semaphore(name))

        bank = [stack.enter_context(nc.psum_tensor(f"bank{i}", [P, 512], F32)) for i in range(8)]
        score_bank, pt_bank, o_bank, r_bank, misc_a, misc_b = bank[0:2], bank[2:4], bank[4], bank[5], bank[6], bank[7]

        ident = sb("ident", [P, P])
        mask_rows = sb("mask_rows", [P, B, S], BF16)
        three_ones = sb("three_ones", [P, P], BF16)
        before = sb("before", [P, P], BF16)
        all_ones = sb("all_ones", [P, P], BF16)
        iota8 = sb("iota8", [P, E])
        sign = sb("sign", [P, 2, E])
        number = sb("number", [P, TILES])
        slot = sb("slot", [P, J])
        middle = sb("middle", [P, E])
        next_row = sb("next_row", [P, 2, E])
        eps_t = sb("eps_t", [P, TILES])
        half_t = sb("half_t", [P, TILES])
        w_in = sb("w_in", [P, 4, D])
        wq_s, wk_s, wv_s, wo_s = (w_in[:, i, :] for i in range(4))
        gate_s = sb("gate_s", [P, E])
        cols = sb("cols", [P, 3])
        q_scale = sb("q_scale", [P, 2])
        q_bias = sb("q_bias", [P, 2])
        bo_b = sb("bo_b", [P, D])
        out_bias = sb("out_bias", [P, D])
        mask_in = sb("mask_in", [B, S])
        mask_f = sb("mask_f", [B, 2, S])
        mask_p = sb("mask_p", [B, 3, S], BF16)
        fc_b = sb("fc_b", [P, E * HC])
        fc_e = [sb(f"fc_e{i}", [P, HC]) for i in range(2)]
        pj_b = sb("pj_b", [P, E, D])

        res = sb("res", [P, TILES, D])
        stats = sb("stats", [P, TILES, 6])
        ln = sb("ln", [P, 4, TILES])
        mean1, rstd1 = ln[:, 0, :], ln[:, 3, :]
        ctx_s = [sb(f"ctx_s{i}", [P, TG, D]) for i in range(2)]
        xn = [sb(f"xn{i}", [P, TG, D]) for i in range(2)]
        xT = sb("xT", [P, TOK])
        cT = sb("cT", [P, TOK])
        kT = sb("kT", [P, TOK])
        q_blk = [sb(f"q_blk{i}", [P, BG, 2, S]) for i in range(2)]
        k_blk = [sb(f"k_blk{i}", [P, PAIRS, TOK]) for i in range(2)]
        v_blk = [sb(f"v_blk{i}", [P, BG, TG, 2, 2 * DH]) for i in range(2)]
        top = sb("top", [P, 4, PAIRS])
        probs = [sb(f"probs{i}", [P, PAIRS, S]) for i in range(4)]
        total = sb("total", [P, 4, PAIRS])
        recip = sb("recip", [P, 4, PAIRS])
        half_rows = sb("half_rows", [P, 2, DH])
        recip_rows = [sb(f"recip_rows{i}", [P, PAIRS, 2, DH]) for i in range(2)]
        pT = [sb(f"pT{i}", [P, 512]) for i in range(2)]
        rT = sb("rT", [P, 512])
        o_mul = sb("o_mul", [P, 4, 2, S])
        oT = [sb(f"oT{i}", [P, TOK]) for i in range(2)]

        row = [sb(f"row{i}", [P, TG, ROW]) for i in range(2)]
        rows_at = [sb(f"rows_at{i}", [P, TG, 2], I32) for i in range(2)]
        stats2 = sb("stats2", [P, TG, 6])
        aggr2 = sb("aggr2", [P, TG, 2])
        rstd2 = sb("rstd2", [P, 2, TG])
        x2T = sb("x2T", [P, TOK])
        logits = sb("logits", [P, TG, E])
        best = sb("best", [P, TG, 8])
        best_at = sb("best_at", [P, TG, 8], U32)
        chosen = sb("chosen", [P, TG, 2, E], BF16)
        signed = sb("signed", [P, TG, 2, E], BF16)
        gap = sb("gap", [P, 3, TG])
        place = sb("place", [P, TG, 2, E])
        place_f = sb("place_f", [P, TG, 2])

        start_i = sb("start_i", [P, E], I32)
        n_first = sb("n_first", [P, E])
        n_all = sb("n_all", [P, E])
        first_f = sb("first_f", [P, E])
        xs = [sb(f"xs{i}", [P, J, ROW]) for i in range(2)]
        fc_s = [sb(f"fc_s{i}", [P, HID]) for i in range(2)]
        pj_s = [sb(f"pj_s{i}", [P, HC, D]) for i in range(2)]
        xsT = sb("xsT", [P, CAP])
        hT = sb("hT", [P, HC, CAP])
        y_s = [k_blk[0][:, 0:3, :].rearrange("p a b -> p (a b)")[:, 0:CAP].rearrange("p (j d) -> p j d", d=D),
               k_blk[0][:, 4:7, :].rearrange("p a b -> p (a b)")[:, 0:CAP].rearrange("p (j d) -> p j d", d=D)]
        y_at = [sb(f"y_at{i}", [P, J], I32) for i in range(2)]
        slot_w = [sb(f"slot_w{i}", [P, J]) for i in range(2)]
        slot_t = sb("slot_t", [P, 4, J])
        y_in = [k_blk[1][:, 2 * i:2 * i + 2, :].rearrange("p k (t d) -> p k t d", d=D) for i in range(4)]
        fill = xs[0]

        names = """w_loaded small_loaded x_loaded0 x_loaded ctx_loaded0 ctx_loaded1 k_placed0 k_placed1 mask_placed
            consts_made fill_made filled setup v_bias_done out_bias_done heads_made inverted ln1_step rstd1_half rstd1_done
            xn_done xT_done cT_done k_done q_done v_done attn_done x2T_done logits_done ranks_done bias_done
            xT_copied cT_copied k_copied q_copied v_copied x2T_copied biased
            scores_done top_done shifted exp_done sum_step recip_done probsT_done probsT_copied
            heads_done recipT_copied o_step res_done ln2_step rstd2_done row_done
            route_step chosen_done gap_exp place_step scattered0 scattered1
            window_step start_done xs_loaded0 xs_loaded1 fc_loaded0 fc_loaded1 pj_loaded0 pj_loaded1
            xsT_done xsT_copied up_done gelu_done down_done slot_step y_done y_step y_scattered0 y_scattered1
            y_loaded sum_done stored""".split()
        s = {n: sem(n) for n in names}
        x_loaded0, ln1_step = s["x_loaded0"], s["ln1_step"]
        ctx_loaded, k_placed = [s["ctx_loaded0"], s["ctx_loaded1"]], [s["k_placed0"], s["k_placed1"]]
        scattered, xs_loaded = [s["scattered0"], s["scattered1"]], [s["xs_loaded0"], s["xs_loaded1"]]
        fc_loaded, pj_loaded = [s["fc_loaded0"], s["fc_loaded1"]], [s["pj_loaded0"], s["pj_loaded1"]]
        y_scattered = [s["y_scattered0"], s["y_scattered1"]]
        in_loaded = [sem(f"y_loaded{i}") for i in range(4)]

        LN1_STEPS, LN2_STEPS, ROUTE_STEPS, PLACE_STEPS, WINDOW_STEPS, SLOT_STEPS = 7, 8, 11, 7, 6, 7

        def groups(engine, body):
            body(0, 0, 0, True, False)
            body(1, 0, 1, False, False)
            with engine.Fori(1, GROUPS // 2 - 1) as i:
                body(2 * i, i, 0, False, False)
                body(2 * i + 1, i, 1, False, False)
            body(GROUPS - 2, GROUPS // 2 - 1, 0, False, False)
            body(GROUPS - 1, GROUPS // 2 - 1, 1, False, True)

        def experts(engine, body):
            body(0, 0, 0)
            body(1, 0, 1)
            with engine.Fori(1, E // 2) as i:
                body(2 * i, i, 0)
                body(2 * i + 1, i, 1)

        block = stack.enter_context(nc.Block())

        @block.sync
        def _(sp):
            def load_ctx(g, par):
                sp.dma_start(ctx_s[par][:, :, :], ctx_v[:, bass.ds(g * TG, TG), :]).then_inc(ctx_loaded[par], 16)

            def place_keys(g, par):
                wait_before(sp, s["k_copied"], g + 1, s["consts_made"])
                for pair in range(PAIRS):
                    r = slice(2 * DH * pair, 2 * DH * (pair + 1))
                    sp.dma_start(k_blk[par][r, pair, :], kT[r, :]).then_inc(k_placed[par], 16)

            sp.dma_start(res[:, 0:TG, :], x_v[:, 0:TG, :]).then_inc(x_loaded0, 16)
            load_ctx(0, 0)
            for i, w in enumerate((wq, wk, wv, wo)):
                sp.dma_start(w_in[:, i, :], w).then_inc(s["w_loaded"], 16)
            sp.dma_start(res[:, TG:TILES, :], x_v[:, TG:TILES, :]).then_inc(s["x_loaded"], 16)
            load_ctx(1, 1)
            sp.wait_ge(s["setup"], 2)
            sp.wait_ge(s["consts_made"], 1)
            for i in range(3):
                sp.dma_start(mask_rows[i:i + 1, :, :], mask_p[:, i, :]).then_inc(s["mask_placed"], 16)
            sp.wait_ge(s["fill_made"], 4)
            place_keys(0, 0)

            def body(g, half, par, first, last):
                if last:
                    return
                if not first:
                    wait_before(sp, s["scores_done"], BG * g, s["consts_made"])
                place_keys(g + 1, 1 - par)

            def loads(g, half, par, first, last):
                if not (last or first):
                    wait_before(sp, s["cT_done"], g, s["consts_made"])
                    load_ctx(g + 1, 1 - par)
                body(g, half, par, first, last)

            groups(sp, loads)

            def load_weights(e, par):
                sp.dma_start(fc_s[par][:, :], c_fc.rearrange("e d h -> d e h")[:, bass.ds(e, 1), :].rearrange("d e h -> d (e h)")
                             ).then_inc(fc_loaded[par], 16)
                sp.dma_start(pj_s[par][:, :, :], c_proj.rearrange("e (c p) d -> p e c d", p=P)[:, bass.ds(e, 1), :, :]
                             .rearrange("p e c d -> p (e c) d")).then_inc(pj_loaded[par], 16)

            def load_window(e, par):
                start = sp.value_load(start_i[0:1, bass.ds(e, 1)], min_val=0, max_val=E * LINE - CAP)
                sp.dma_start(xs[par][:, :, :].rearrange("p j r -> p (j r)"),
                             lines[bass.ds(start, CAP), :].rearrange("(p j) r -> p (j r)", p=P)).then_inc(xs_loaded[par], 16)

            load_weights(0, 0)
            load_weights(1, 1)
            sp.wait_ge(s["start_done"], 1)
            for par in range(2):
                sp.wait_ge(scattered[par], 16 * 2 * TG * GROUPS // 2)
            load_window(0, 0)
            load_window(1, 1)
            with sp.Fori(0, E // 2 - 1) as i:
                for par in range(2):
                    e = 2 * i + par
                    wait_before(sp, s["down_done"], J * (e + 1), s["consts_made"])
                    load_weights(e + 2, par)
                    wait_before(sp, s["slot_step"], SLOT_STEPS * (e + 1), s["consts_made"])
                    wait_before(sp, s["xsT_done"], 3 * (e + 1), s["consts_made"])
                    load_window(e + 2, par)

            for par in range(2):
                sp.wait_ge(y_scattered[par], 16 * J * E // 2)
            for g in range(GROUPS):
                if g >= 4:
                    sp.wait_ge(s["sum_done"], 2 * (g - 3))
                for k in range(2):
                    sp.dma_start(y_in[g % 4][:, k], table_v[:, k, g * TG:(g + 1) * TG, :]).then_inc(in_loaded[g % 4], 16)
                if g >= 2:
                    sp.wait_ge(s["sum_done"], 2 * (g - 1))
                    sp.dma_start(out_v[:, (g - 2) * TG:(g - 1) * TG, :], res[:, (g - 2) * TG:(g - 1) * TG, :]).then_inc(s["stored"], 16)
            for g in range(GROUPS, GROUPS + 2):
                sp.wait_ge(s["sum_done"], 2 * (g - 1))
                sp.dma_start(out_v[:, (g - 2) * TG:(g - 1) * TG, :], res[:, (g - 2) * TG:(g - 1) * TG, :]).then_inc(s["stored"], 16)
            sp.wait_ge(s["stored"], 16 * GROUPS)

        @block.gpsimd
        def _(pool):
            pool.memset(ident[:, :], 0.0).then_inc(s["consts_made"], 1)
            pool.memset(before[:, :], 1.0).then_inc(s["consts_made"], 1)
            pool.wait_ge(s["consts_made"], 2)
            pool.affine_select(out=ident[:, :], in_=ident[:, :], compare_op=ALU.not_equal, fill=1.0, base=0,
                               pattern=[[-1, P]], channel_multiplier=1).then_inc(s["consts_made"], 1)
            pool.affine_select(out=before[:, :], in_=before[:, :], compare_op=ALU.is_gt, fill=0.0, base=0,
                               pattern=[[1, P]], channel_multiplier=-1).then_inc(s["consts_made"], 1)
            pool.memset(eps_t[:, :], EPS)
            pool.memset(half_t[:, :], -0.5).then_inc(s["consts_made"], 1)
            pool.wait_ge(s["consts_made"], 5)

            def rstd(variance, half, out_, n, gate, done):
                pool.tensor_tensor(half, variance, eps_t[:, 0:n], ALU.add).then_inc(s["rstd1_half"], 1)
                pool.wait_ge(s["rstd1_half"], gate)
                pool.tensor_tensor(out_, half, half_t[:, 0:n], ALU.pow).then_inc(done, 1)

            pool.wait_ge(ln1_step, LN1_STEPS)
            rstd(ln[:, 1, 0:TG], ln[:, 2, 0:TG], ln[:, 3, 0:TG], TG, 1, s["rstd1_done"])
            pool.iota(iota8[:, :], pattern=[[1, E]], base=0, channel_multiplier=0, allow_small_or_imprecise_dtypes=True)
            pool.iota(next_row[:, :, :], pattern=[[1, 2], [LINE, E]], base=N - 1, channel_multiplier=0, allow_small_or_imprecise_dtypes=True)
            pool.iota(middle[:, :], pattern=[[LINE, E]], base=N, channel_multiplier=0, allow_small_or_imprecise_dtypes=True)
            pool.iota(number[:, :], pattern=[[P, TILES]], base=0, channel_multiplier=1, allow_small_or_imprecise_dtypes=True)
            pool.iota(slot[:, :], pattern=[[1, J]], base=0, channel_multiplier=J, allow_small_or_imprecise_dtypes=True)
            pool.memset(all_ones[:, :], 1.0)
            pool.memset(sign[:, 0, :], -1.0)
            pool.memset(sign[:, 1, :], 1.0).then_inc(s["consts_made"], 1)
            pool.wait_ge(ln1_step, 2 * LN1_STEPS)
            rstd(ln[:, 1, TG:TILES], ln[:, 2, TG:TILES], ln[:, 3, TG:TILES], TILES - TG, 2, s["rstd1_done"])
            pool.wait_ge(s["fill_made"], 6)
            for e in range(E):
                pool.dma_start(lines_fill[:, e, :], fill[:, :, :].rearrange("p j r -> p (j r)")).then_inc(s["filled"], 16)
            for k in range(2):
                for t in range(0, TILES, 8):
                    pool.dma_start(table_v[:, k, t:t + 8, :], fill[:, 0:8, 0:D]).then_inc(s["filled"], 16)

            def route(g, half, par):
                wait_before(pool, s["place_step"], PLACE_STEPS * (g + 1), s["consts_made"])
                for t in range(TG):
                    for k in range(2):
                        pool.indirect_dma_start(
                            lines, bass.IndirectOffsetOnAxis(ap=rows_at[par][:, t, k:k + 1], axis=0), row[par][:, t, :], None,
                            bounds_check=E * LINE - 1, oob_is_err=False).then_inc(scattered[par], 16)

            def power2(g):
                pool.wait_ge(s["ln2_step"], LN2_STEPS * (g + 1))
                rstd(aggr2[:, :, 1], rstd2[:, 0, :], rstd2[:, 1, :], TG, g + 3, s["rstd2_done"])

            def bias_residual(g):
                pool.wait_ge(s["xn_done"], g + 1)
                r = res[:, bass.ds(g * TG, TG), :]
                pool.tensor_tensor(r, r, out_bias[:, :].rearrange("p (a d) -> p a d", a=1).to_broadcast([P, TG, D]), ALU.add).then_inc(s["biased"], 1)

            pool.wait_ge(s["out_bias_done"], 2)

            def body(g, half, par, first, last):
                if not first:
                    power2(g - 1)
                bias_residual(g)
                if first:
                    pool.wait_ge(s["filled"], 16 * (E + 2 * TILES // 8))
                else:
                    route(g - 1, half, 1 - par)

            groups(pool, body)
            power2(GROUPS - 1)
            route(GROUPS - 1, 0, 1)

            def scatter(e, half, par):
                pool.wait_ge(s["slot_step"], SLOT_STEPS * (e + 1))
                for j in range(J):
                    if j % 4 == 0:
                        wait_before(pool, s["y_done"], 3 * e + j // 4 + 1, s["consts_made"])
                    pool.indirect_dma_start(
                        table, bass.IndirectOffsetOnAxis(ap=y_at[par][:, j:j + 1], axis=0), y_s[par][:, j, :], None,
                        bounds_check=2 * N - 1, oob_is_err=False).then_inc(y_scattered[par], 16)

            experts(pool, scatter)

        @block.scalar
        def _(act):
            act.dma_start(gate_s[:, :], gate_w).then_inc(s["small_loaded"], 16)
            act.dma_start(mask_in[:, :], mask).then_inc(s["small_loaded"], 16)
            for i, b_ in enumerate((bq, bk, bv)):
                act.dma_start(cols[:, i:i + 1], b_.rearrange("(p a) -> p a", a=1)).then_inc(s["small_loaded"], 16)
            act.dma_start(bo_b[:, :], bo.rearrange("(a d) -> a d", a=1).to_broadcast([P, D])).then_inc(s["small_loaded"], 16)
            act.dma_start(fc_b[:, :], fc_bias).then_inc(s["small_loaded"], 16)
            act.dma_start(pj_b[:, :, :], proj_bias.rearrange("e a d -> a e d").to_broadcast([P, E, D])).then_inc(s["small_loaded"], 16)

            def copy(dst, src, done, **bias):
                act.activation(dst, src, ACT.Identity, **bias).then_inc(done, 1)

            def copy_cT(g):
                act.wait_ge(s["cT_done"], g + 1)
                wait_later(act, s["v_done"], g)
                copy(cT[:, :], misc_a[:, :], s["cT_copied"])

            def copy_xT(g):
                act.wait_ge(s["xT_done"], g + 1)
                wait_later(act, s["q_done"], g)
                copy(xT[:, :], misc_b[:, :], s["xT_copied"])

            def copy_k(g, half, par):
                act.wait_ge(s["k_done"], g + 1)
                wait_later(act, k_placed[1 - par], 16 * PAIRS * (half if par == 0 else half + 1))
                copy(kT[:, :], misc_b[:, :], s["k_copied"], bias=cols[:, 1:2])

            def copy_q(g, par):
                act.wait_ge(s["q_done"], g + 1)
                for h2 in range(2):
                    copy(q_blk[par][:, :, h2, :], misc_a[:, :].rearrange("p (b q) -> p b q", b=BG), s["q_copied"],
                         bias=q_bias[:, h2:h2 + 1], scale=q_scale[:, h2:h2 + 1])

            def copy_v(g, par):
                act.wait_ge(s["v_done"], g + 1)
                for pp in range(2):
                    r = slice(S * pp, S * (pp + 1))
                    copy(v_blk[par][r, :, :, pp, :].rearrange("k b j c -> k (b j) c"),
                         misc_b[r, :].rearrange("k (a c) -> k a c", c=2 * DH), s["v_copied"])

            def exp(n, k):
                act.wait_ge(s["shifted"], n + 1)
                act.activation(probs[k % 4][:, :, :], probs[k % 4][:, :, :], ACT.Exp).then_inc(s["exp_done"], 1)

            def copy_probsT(n, b, first):
                act.wait_ge(s["probsT_done"], n + 1)
                if not (first and b < 2):
                    act.wait_ge(s["heads_done"], n - 1)
                copy(pT[b % 2][:, :], pt_bank[b % 2][:, :], s["probsT_copied"])

            def copy_recipT(quad, first):
                act.wait_ge(s["heads_done"], 4 * (quad + 1))
                if not first:
                    act.wait_ge(s["o_step"], 2 * quad)
                copy(rT[:, :], r_bank[:, :], s["recipT_copied"])

            def copy_x2T(g):
                act.wait_ge(s["x2T_done"], g + 1)
                wait_later(act, s["logits_done"], g)
                copy(x2T[:, :], misc_a[:, :], s["x2T_copied"])

            def exp_gap(g):
                act.wait_ge(s["chosen_done"], g + 1)
                act.activation(gap[:, 1, :], gap[:, 0, :], ACT.Exp).then_inc(s["gap_exp"], 1)

            copy_xT(0)
            copy_cT(0)
            act.wait_ge(s["small_loaded"], 16 * 8)
            copy_k(0, 0, 0)
            act.wait_ge(s["setup"], 4)
            copy_q(0, 0)
            act.wait_ge(s["fill_made"], 6)
            copy_v(0, 0)
            exp(0, 0)

            def body(g, half, par, first, last):
                for b in range(BG):
                    n = BG * g + b
                    if b == 1 and not first:
                        copy_recipT(2 * g - 1, False)
                    if b == 1 and not last:
                        copy_cT(g + 1)
                    if b == 2 and not last:
                        copy_xT(g + 1)
                    if b == 3 and not last:
                        copy_k(g + 1, half if par == 0 else half + 1, 1 - par)
                    copy_probsT(n, b, first)
                    if b == 4 and not last:
                        copy_q(g + 1, 1 - par)
                    if b == 5:
                        copy_recipT(2 * g, first)
                        if not last:
                            copy_v(g + 1, 1 - par)
                        if not first:
                            copy_x2T(g - 1)
                    if not (last and b == BG - 1):
                        exp(n + 1, b + 1)
                    if b == 7 and not first:
                        exp_gap(g - 1)

            groups(act, body)
            copy_recipT(2 * GROUPS - 1, False)
            copy_x2T(GROUPS - 1)
            exp_gap(GROUPS - 1)

            def gelus(e, half, par):
                act.wait_ge(s["bias_done"], e + 1)
                for c in range(HC):
                    for i, (a, b) in enumerate(((0, 512), (512, 1024), (1024, CAP))):
                        act.wait_ge(s["up_done"], 3 * HC * e + 3 * c + i + 1)
                        act.activation(hT[:, c, a:b], bank[(3 * c + i) % 4][:, 0:b - a], ACT.Gelu,
                                       bias=fc_e[par][:, c:c + 1]).then_inc(s["gelu_done"], 1)

            experts(act, gelus)

        @block.vector
        def _(dve):
            v = nc.vector
            v.memset(mask_rows[:, :, :], 0.0).then_inc(s["setup"], 1)

            def ln1(t0, t1, turn):
                ch = Chain(dve, ln1_step, LN1_STEPS, turn)
                m, var, tmp = ln[:, 0, t0:t1], ln[:, 1, t0:t1], ln[:, 2, t0:t1]
                st = stats[:, t0:t1, :]
                ch.step(v.tensor_tensor(m, st[:, :, 1], st[:, :, 4], ALU.add))
                ch.step(v.tensor_scalar(m, m, 0.5, None, ALU.mult))
                ch.step(v.tensor_tensor(tmp, st[:, :, 1], m, ALU.subtract))
                ch.step(v.tensor_tensor(tmp, tmp, tmp, ALU.mult))
                ch.step(v.tensor_tensor(var, st[:, :, 2], st[:, :, 5], ALU.add))
                ch.step(v.tensor_scalar(var, var, 1.0 / D, None, ALU.mult))
                ch.step(v.tensor_tensor(var, var, tmp, ALU.add))
                ch.end()

            def normalise1(g, par):
                wait_later(dve, s["xT_done"], g - 1)
                for t in range(TG):
                    at = g * TG + t
                    last = v.tensor_scalar(xn[par][:, t, :], res[:, bass.ds(at, 1), :].rearrange("p a d -> p (a d)"),
                                           mean1[:, bass.ds(at, 1)], rstd1[:, bass.ds(at, 1)], ALU.subtract, ALU.mult)
                last.then_inc(s["xn_done"], 1)

            dve.wait_ge(x_loaded0, 16)
            for t in range(TG):
                v.bn_stats(stats[:, t, :], res[:, t, :]).then_inc(s["v_bias_done"], 1)
            dve.wait_ge(s["v_bias_done"], TG)
            ln1(0, TG, 0)
            dve.wait_ge(s["small_loaded"], 16 * 8)
            mch = Chain(dve, s["window_step"], 6, 0)
            mch.step(v.tensor_scalar(mask_f[:, 0, :], mask_in[:, :], -1.0, 1.0, ALU.mult, ALU.add))
            mch.step(v.tensor_scalar(mask_f[:, 0, :], mask_f[:, 0, :], -1.0e30, None, ALU.mult))
            mch.step(v.tensor_copy(mask_p[:, 0, :], mask_f[:, 0, :]))
            mch.step(v.tensor_tensor(mask_f[:, 1, :], mask_f[:, 0, :], mask_p[:, 0, :], ALU.subtract))
            mch.step(v.tensor_copy(mask_p[:, 1, :], mask_f[:, 1, :]))
            mch.step(v.tensor_tensor(mask_f[:, 0, :], mask_f[:, 1, :], mask_p[:, 1, :], ALU.subtract))
            v.tensor_copy(mask_p[:, 2, :], mask_f[:, 0, :]).then_inc(s["setup"], 1)
            dve.wait_ge(s["rstd1_done"], 1)
            normalise1(0, 0)
            dve.wait_ge(s["consts_made"], 5)
            v.reduce_sum(q_scale[:, :], ident[:, :].rearrange("p (a h d) -> p h a d", h=2, d=DH), AX.XY).then_inc(s["out_bias_done"], 1)
            dve.wait_ge(s["out_bias_done"], 1)
            v.tensor_scalar(q_scale[:, :], q_scale[:, :], SCALE, None, ALU.mult).then_inc(s["setup"], 1)
            dve.wait_ge(s["setup"], 3)
            v.tensor_scalar(q_bias[:, :], q_scale[:, :], cols[:, 0:1], None, ALU.mult).then_inc(s["setup"], 1)
            v.memset(three_ones[:, :], 0.0).then_inc(s["fill_made"], 1)
            dve.wait_ge(s["fill_made"], 1)
            v.memset(three_ones[0:3, :], 1.0).then_inc(s["fill_made"], 1)
            v.memset(k_blk[0][:, :, :], 0.0).then_inc(s["fill_made"], 1)
            v.memset(k_blk[1][:, :, :], 0.0).then_inc(s["fill_made"], 1)
            for i in range(2):
                v.memset(v_blk[i][:, :, :, :, :], 0.0)
            v.memset(half_rows[:, :, :], 0.0).then_inc(s["heads_made"], 1)
            dve.wait_ge(s["heads_made"], 1)
            for h2 in range(2):
                v.memset(half_rows[S * h2:S * (h2 + 1), h2, :], 1.0).then_inc(s["heads_made"], 1)
            dve.wait_ge(s["heads_made"], 3)
            v.memset(fill[:, :, :], 0.0).then_inc(s["fill_made"], 1)
            dve.wait_ge(s["fill_made"], 5)
            v.memset(fill[:, :, D + 2:D + 3], NOWHERE).then_inc(s["fill_made"], 1)
            dve.wait_ge(s["x_loaded"], 16)
            with dve.Fori(1, GROUPS) as g:
                for t in range(TG):
                    v.bn_stats(stats[:, bass.ds(g * TG + t, 1), :].rearrange("p a c -> p (a c)"),
                               res[:, bass.ds(g * TG + t, 1), :].rearrange("p a d -> p (a d)")).then_inc(s["v_bias_done"], 1)
            dve.wait_ge(s["v_bias_done"], TILES)
            ln1(TG, TILES, 1)
            dve.wait_ge(s["attn_done"], 1)
            v.tensor_tensor(out_bias[:, :], misc_a[:, 0:D], bo_b[:, :], ALU.add).then_inc(s["out_bias_done"], 1)

            def shift(n, k):
                dve.wait_ge(s["scores_done"], n + 1)
                sc = score_bank[k % 2][:, :].rearrange("p (a k) -> p a k", k=S)
                v.reduce_max(top[:, k % 4, :], sc, AX.X).then_inc(s["top_done"], 1)
                wait_later(dve, s["probsT_done"], n - 3)
                dve.wait_ge(s["top_done"], n + 1)
                v.tensor_tensor(probs[k % 4][:, :, :], sc,
                                top[:, k % 4, :].rearrange("p (a b) -> p a b", b=1).to_broadcast([P, PAIRS, S]),
                                ALU.subtract).then_inc(s["shifted"], 1)

            def invert(n, k, first):
                dve.wait_ge(s["exp_done"], n + 1)
                v.reduce_sum(total[:, k % 4, :], probs[k % 4][:, :, :], AX.X).then_inc(s["sum_step"], 1)
                dve.wait_ge(s["sum_step"], n + 1)
                v.reciprocal(recip[:, k % 4, :], total[:, k % 4, :]).then_inc(s["inverted"], 1)
                if not (first and k < 2):
                    dve.wait_ge(s["heads_done"], n - 1)
                dve.wait_ge(s["inverted"], n + 1)
                v.tensor_tensor(recip_rows[k % 2][:, :, :, :].rearrange("p a h c -> p a (h c)"),
                                recip[:, k % 4, :].rearrange("p (a b) -> p a b", b=1).to_broadcast([P, PAIRS, 2 * DH]),
                                half_rows[:, :, :].rearrange("p (b h) c -> p b (h c)", b=1).to_broadcast([P, PAIRS, 2 * DH]),
                                ALU.mult).then_inc(s["recip_done"], 1)

            def join_heads(quad, par, q2):
                dve.wait_ge(s["recipT_copied"], quad + 1)
                v.tensor_tensor(o_mul[:, :, :, :].rearrange("p b h q -> p (b h q)"), o_bank[:, :], rT[:, :], ALU.mult).then_inc(s["o_step"], 1)
                dve.wait_ge(s["o_step"], 2 * quad + 1)
                v.tensor_tensor(oT[par][:, q2 * 256:(q2 + 1) * 256].rearrange("p (b q) -> p b q", b=4),
                                o_mul[:, :, 0, :], o_mul[:, :, 1, :], ALU.add).then_inc(s["o_step"], 1)

            def residual(g):
                dve.wait_ge(s["attn_done"], g + 2)
                dve.wait_ge(s["biased"], g + 1)
                r = res[:, bass.ds(g * TG, TG), :]
                v.tensor_tensor(r, misc_a[:, :].rearrange("p (t d) -> p t d", t=TG), r, ALU.add).then_inc(s["res_done"], 1)
                wait_before(dve, s["res_done"], g + 1, s["setup"])
                ch = Chain(dve, s["ln2_step"], LN2_STEPS, g)
                for t in range(TG):
                    ch.mark(v.bn_stats(stats2[:, t, :], res[:, bass.ds(g * TG + t, 1), :].rearrange("p a d -> p (a d)")))
                wait_before(dve, s["ln2_step"], ch.base + TG, s["setup"])
                for t in range(TG):
                    ch.mark(v.bn_aggr(aggr2[:, t, :], stats2[:, t, :]))
                ch.end()

            def normalise2(g, half, par):
                dve.wait_ge(s["rstd2_done"], g + 1)
                wait_later(dve, scattered[par], 16 * 2 * TG * half)
                for t in range(TG):
                    last = v.tensor_scalar(row[par][:, t, 0:D], res[:, bass.ds(g * TG + t, 1), :].rearrange("p a d -> p (a d)"),
                                           aggr2[:, t, 0:1], rstd2[:, 1, t:t + 1], ALU.subtract, ALU.mult)
                last.then_inc(s["row_done"], 1)

            def choose(g):
                dve.wait_ge(s["logits_done"], g + 1)
                ch = Chain(dve, s["route_step"], ROUTE_STEPS, g)
                ch.mark(v.tensor_copy(logits[:, :, :].rearrange("p t e -> p (t e)"), misc_b[:, 0:TG * E]))
                wait_before(dve, s["route_step"], ch.base + 1, s["setup"])
                for t in range(TG):
                    ch.mark(v.max(best[:, t, :], logits[:, t, :]))
                wait_before(dve, s["route_step"], ch.base + 1 + TG, s["setup"])
                for t in range(TG):
                    ch.mark(v.max_index(best_at[:, t, :], best[:, t, :], logits[:, t, :]))
                dve.wait_ge(s["route_step"], ch.base + 1 + 2 * TG)
                wait_later(dve, s["ranks_done"], g)
                ch.step(v.tensor_tensor(chosen[:, :, :, :],
                                        best_at[:, :, 0:2].rearrange("p t (k a) -> p t k a", a=1).to_broadcast([P, TG, 2, E]),
                                        iota8[:, :].rearrange("p (a b e) -> p a b e", a=1, b=1).to_broadcast([P, TG, 2, E]), ALU.is_equal))
                v.tensor_tensor(gap[:, 0, :], best[:, :, 1], best[:, :, 0], ALU.subtract).then_inc(s["chosen_done"], 1)
                ch.mark(v.tensor_tensor(signed[:, :, :, :].rearrange("p t k e -> p t (k e)"), chosen[:, :, :, :].rearrange("p t k e -> p t (k e)"),
                                        sign[:, :, :].rearrange("p k e -> p (k e)").rearrange("p (a c) -> p a c", a=1).to_broadcast([P, TG, 2 * E]), ALU.mult))
                ch.end()

            def place_rows(g, half, par):
                dve.wait_ge(s["ranks_done"], g + 1)
                ch = Chain(dve, s["place_step"], PLACE_STEPS, g)
                nr = next_row[:, :, :].rearrange("p k e -> p (k e)")
                ch.step(v.tensor_tensor(place[:, :, :, :].rearrange("p t k e -> p t (k e)"),
                                        misc_a[:, 0:TG * 2 * E].rearrange("p (t c) -> p t c", t=TG),
                                        nr.rearrange("p (a c) -> p a c", a=1).to_broadcast([P, TG, 2 * E]), ALU.add))
                ch.step(v.tensor_tensor(place[:, :, :, :], place[:, :, :, :], chosen[:, :, :, :], ALU.mult))
                ch.step(v.reduce_sum(place_f[:, :, :], place[:, :, :, :], AX.X))
                v.tensor_copy(rows_at[par][:, :, :], place_f[:, :, :])
                ch.mark(v.tensor_tensor(nr, misc_a[:, TG * 2 * E:(TG + 1) * 2 * E], nr, ALU.add))
                dve.wait_ge(s["gap_exp"], g + 1)
                ch.step(v.tensor_scalar(gap[:, 2, :], gap[:, 1, :], 1.0, None, ALU.add))
                ch.step(v.reciprocal(row[par][:, :, D], gap[:, 2, :]))
                v.tensor_copy(row[par][:, :, D + 2], number[:, bass.ds(g * TG, TG)])
                ch.mark(v.tensor_tensor(row[par][:, :, D + 1], row[par][:, :, D], gap[:, 1, :], ALU.mult))
                ch.end()

            shift(0, 0)

            def body(g, half, par, first, last):
                for b in range(BG):
                    n = BG * g + b
                    if not (last and b == BG - 1):
                        shift(n + 1, b + 1)
                    if b == 0 and not last:
                        if first:
                            dve.wait_ge(s["rstd1_done"], 2)
                        normalise1(g + 1, 1 - par)
                    invert(n, b, first)
                    if b == 1 and not first:
                        join_heads(2 * g - 1, 1 - par, 1)
                    if b == 3 and not first:
                        residual(g - 1)
                    if b == 4 and not first:
                        normalise2(g - 1, half if par == 1 else half - 1, 1 - par)
                    if b == 5:
                        join_heads(2 * g, par, 0)
                    if b == 6 and not first:
                        choose(g - 1)
                    if b == 7 and not first:
                        place_rows(g - 1, half, 1 - par)

            groups(dve, body)
            join_heads(2 * GROUPS - 1, 1, 1)
            residual(GROUPS - 1)
            normalise2(GROUPS - 1, GROUPS // 2 - 1, 1)
            choose(GROUPS - 1)
            place_rows(GROUPS - 1, 0, 1)

            wch = Chain(dve, s["window_step"], WINDOW_STEPS, 1)
            wch.step(v.tensor_scalar(first_f[:, :], middle[:, :], -float(CAP), None, ALU.add))
            wch.step(v.tensor_scalar(n_all[:, :], next_row[:, 0, :], 1.0, None, ALU.add))
            wch.step(v.tensor_tensor(first_f[:, :], first_f[:, :], n_all[:, :], ALU.max))
            v.tensor_copy(start_i[:, :], first_f[:, :]).then_inc(s["start_done"], 1)
            wch.step(v.tensor_tensor(n_first[:, :], middle[:, :], first_f[:, :], ALU.subtract))
            wch.step(v.tensor_tensor(n_all[:, :], next_row[:, 1, :], middle[:, :], ALU.subtract))
            wch.step(v.tensor_tensor(n_all[:, :], n_all[:, :], n_first[:, :], ALU.add))
            wch.end()

            def expert(e, half, par):
                def copy_xsT(i):
                    dve.wait_ge(s["xsT_done"], 3 * e + i + 1)
                    a, b = 512 * i, min(512 * (i + 1), CAP)
                    v.tensor_copy(xsT[:, a:b], bank[4 + i % 2][:, 0:b - a]).then_inc(s["xsT_copied"], 1)

                wait_later(dve, s["up_done"], 3 * HC * e)
                v.tensor_copy(fc_e[par][:, :], fc_b[:, bass.ds(e * HC, HC)]).then_inc(s["bias_done"], 1)
                for i in range(3):
                    copy_xsT(i)
                wait_later(dve, y_scattered[par], 16 * J * half)
                dve.wait_ge(xs_loaded[par], 16 * (half + 1))
                w0, w1, num = (xs[par][:, :, D + i] for i in range(3))
                sel, diff, num2, none = (slot_t[:, i, :] for i in range(4))
                ch = Chain(dve, s["slot_step"], SLOT_STEPS, e)
                ch.mark(v.tensor_scalar(sel, slot[:, :], n_first[:, bass.ds(e, 1)], None, ALU.is_lt))
                ch.mark(v.tensor_scalar(none, slot[:, :], n_all[:, bass.ds(e, 1)], NOWHERE, ALU.is_ge, ALU.mult))
                ch.step(v.tensor_tensor(diff, w0, w1, ALU.subtract))
                ch.step(v.tensor_tensor(diff, diff, sel, ALU.mult))
                ch.mark(v.tensor_tensor(slot_w[par][:, :], diff, w1, ALU.add))
                ch.step(v.scalar_tensor_tensor(num2, sel, -float(N), num, ALU.mult, ALU.add))
                ch.mark(v.scalar_tensor_tensor(y_at[par][:, :], num2, float(N), none, ALU.add, ALU.add))
                dve.wait_ge(s["slot_step"], ch.base + SLOT_STEPS)
                ch.end()
                for i in range(3):
                    j0, j1 = 4 * i, min(4 * i + 4, J)
                    n = j1 - j0
                    dve.wait_ge(s["down_done"], J * e + j1)
                    v.tensor_tensor(y_s[par][:, j0:j1, :], bank[6 + i % 2][:, 0:n * D].rearrange("p (j d) -> p j d", j=n),
                                    pj_b[:, bass.ds(e, 1), :].to_broadcast([P, n, D]), ALU.add).then_inc(s["y_step"], 1)
                    dve.wait_ge(s["y_step"], 3 * e + i + 1)
                    v.tensor_tensor(y_s[par][:, j0:j1, :], y_s[par][:, j0:j1, :],
                                    slot_w[par][:, j0:j1].rearrange("p (j a) -> p j a", a=1).to_broadcast([P, n, D]), ALU.mult).then_inc(s["y_done"], 1)

            experts(dve, expert)

            for g in range(GROUPS):
                dve.wait_ge(in_loaded[g % 4], 32 * (g // 4 + 1))
                for k in range(2):
                    r = res[:, g * TG:(g + 1) * TG, :]
                    v.tensor_tensor(r, r, y_in[g % 4][:, k], ALU.add).then_inc(s["sum_done"], 1)
                    if k == 0:
                        dve.wait_ge(s["sum_done"], 2 * g + 1)

        @block.tensor
        def _(pe):
            mm = nc.tensor.matmul

            def transposed(dst, src, done):
                for t in range(TG):
                    last = nc.tensor.transpose(dst[:, t * P:(t + 1) * P], src[:, t, 0:D], ident[:, :])
                last.then_inc(done, 1)

            def task_cT(g, par, ctx_count):
                pe.wait_ge(ctx_loaded[par], 16 * ctx_count)
                transposed(misc_a, ctx_s[par], s["cT_done"])

            def task_xT(g, par):
                pe.wait_ge(s["xn_done"], g + 1)
                transposed(misc_b, xn[par], s["xT_done"])

            def task_k(g):
                pe.wait_ge(s["cT_copied"], g + 1)
                pe.wait_ge(s["xT_copied"], g + 1)
                mm(misc_b[:, :], wk_s, cT[:, :], start=True, stop=True).then_inc(s["k_done"], 1)

            def task_q(g):
                pe.wait_ge(s["xT_copied"], g + 1)
                mm(misc_a[:, :], wq_s, xT[:, :], start=True, stop=True).then_inc(s["q_done"], 1)

            def task_v(g):
                pe.wait_ge(s["k_copied"], g + 1)
                w = wv_s.rearrange("p (j a c) -> p j a c", a=2, c=2 * DH)
                for b in range(BG):
                    for pp in range(2):
                        last = mm(misc_b[S * pp:S * (pp + 1), b * S:(b + 1) * S].rearrange("k (j c) -> k j c", j=TG),
                                  cT[:, b * S:(b + 1) * S], w[:, :, pp, :], start=True, stop=True)
                last.then_inc(s["v_done"], 1)

            def task_attn(g, par):
                pe.wait_ge(s["o_step"], 4 * (g + 1))
                for t in range(TG):
                    last = mm(misc_a[:, t * D:(t + 1) * D], oT[par][:, t * P:(t + 1) * P], wo_s, start=True, stop=True)
                last.then_inc(s["attn_done"], 1)

            def task_x2T(g, par):
                pe.wait_ge(s["row_done"], g + 1)
                transposed(misc_a, row[par], s["x2T_done"])

            def task_logits(g):
                pe.wait_ge(s["x2T_copied"], g + 1)
                for t in range(TG):
                    last = mm(misc_b[:, t * E:(t + 1) * E], x2T[:, t * P:(t + 1) * P], gate_s[:, :], start=True, stop=True)
                last.then_inc(s["logits_done"], 1)

            def task_ranks(g):
                pe.wait_ge(s["route_step"], ROUTE_STEPS * (g + 1))
                c = 2 * E
                sg = signed[:, :, :, :].rearrange("p t k e -> p (t k e)")
                mm(misc_a[:, 0:TG * c], before[:, :], sg, start=True, stop=False, skip_group_check=True)
                for d in range(1, TG):
                    mm(misc_a[:, d * c:TG * c], all_ones[:, :], sg[:, 0:(TG - d) * c], start=False, stop=False, skip_group_check=True)
                for t in range(TG):
                    last = mm(misc_a[:, TG * c:(TG + 1) * c], all_ones[:, :], sg[:, t * c:(t + 1) * c],
                              start=False, stop=t == TG - 1, skip_group_check=True)
                last.then_inc(s["ranks_done"], 1)

            def scores(n, b, par):
                wait_later(pe, s["shifted"], n - 1)
                m = mask_rows[:, bass.ds(n, 1), :].to_broadcast([P, PAIRS, S])
                bank_ = score_bank[b % 2][:, :].rearrange("p (a k) -> p a k", k=S)
                mm(bank_, three_ones[:, :], m, start=True, stop=False)
                mm(bank_, q_blk[par][:, b, :, :].rearrange("p h q -> p (h q)"), k_blk[par][:, :, b * S:(b + 1) * S],
                   start=False, stop=True).then_inc(s["scores_done"], 1)

            def scores_first(n, half, par):
                pe.wait_ge(s["q_copied"], 2 * (2 * half + par + 1))
                pe.wait_ge(k_placed[par], 16 * PAIRS * (half + 1))
                scores(n, 0, par)

            def transpose_probs(n, b, first):
                pe.wait_ge(s["exp_done"], n + 1)
                if not (first and b < 2):
                    pe.wait_ge(s["probsT_copied"], n - 1)
                for j in range(4):
                    last = nc.tensor.transpose(pt_bank[b % 2][:, j * P:(j + 1) * P],
                                               probs[b % 4][:, 2 * j:2 * j + 2, :].rearrange("p a k -> p (a k)"), ident[:, :])
                last.then_inc(s["probsT_done"], 1)

            def heads(n, b, par, quads_joined):
                pe.wait_ge(s["probsT_copied"], n + 1)
                if quads_joined is not None:
                    pe.wait_ge(s["o_step"], 2 * quads_joined)
                q = b % 4
                for j in range(4):
                    mm(o_bank[32 * j:32 * (j + 1), q * P:(q + 1) * P], v_blk[par][:, b, j, :, :].rearrange("k a c -> k (a c)"),
                       pT[b % 2][:, j * P:(j + 1) * P], start=True, stop=True)
                pe.wait_ge(s["recip_done"], n + 1)
                nc.tensor.transpose(r_bank[:, q * P:(q + 1) * P], recip_rows[b % 2][:, :, :, :].rearrange("p a h c -> p (a h c)"),
                                    ident[:, :]).then_inc(s["heads_done"], 1)

            pe.wait_ge(s["consts_made"], 5)
            task_xT(0, 0)
            task_cT(0, 0, 1)
            pe.wait_ge(s["w_loaded"], 16 * 4)
            task_k(0)
            pe.wait_ge(s["cT_copied"], 1)
            task_q(0)
            task_v(0)
            pe.wait_ge(s["small_loaded"], 16 * 8)
            pe.wait_ge(s["q_copied"], 2)
            mm(misc_a[:, 0:D], cols[:, 2:3].to_broadcast([P, P]), wo_s, start=True, stop=True).then_inc(s["attn_done"], 1)
            pe.wait_ge(s["v_copied"], 2)
            pe.wait_ge(s["fill_made"], 4)
            pe.wait_ge(s["mask_placed"], 48)
            scores_first(0, 0, 0)

            def body(g, half, par, first, last):
                nh, np_ = (half, 1) if par == 0 else (half + 1, 0)
                for b in range(BG):
                    n = BG * g + b
                    if b < BG - 1:
                        scores(n + 1, b + 1, par)
                    elif not last:
                        scores_first(n + 1, nh, np_)
                    if b == 1 and not last:
                        if first:
                            pe.wait_ge(s["out_bias_done"], 2)
                        else:
                            wait_later(pe, s["place_step"], PLACE_STEPS * (g - 1))
                        task_cT(g + 1, 1 - par, nh + 1)
                    if b == 2:
                        if not last:
                            wait_later(pe, s["route_step"], ROUTE_STEPS * (g - 1))
                            pe.wait_ge(s["v_copied"], 2 * (g + 1))
                            task_xT(g + 1, 1 - par)
                            pe.wait_ge(s["cT_copied"], g + 2)
                        if not first:
                            if last:
                                pe.wait_ge(s["place_step"], PLACE_STEPS * (g - 1))
                            task_attn(g - 1, 1 - par)
                    if b == 3 and not last:
                        task_k(g + 1)
                    if b == 4 and not last:
                        wait_later(pe, s["res_done"], g)
                        task_q(g + 1)
                    if b == 5:
                        if not last:
                            task_v(g + 1)
                            pe.wait_ge(s["q_copied"], 2 * (g + 2))
                        if not first:
                            if last:
                                pe.wait_ge(s["res_done"], g)
                            task_x2T(g - 1, 1 - par)
                    if b == 6 and not first:
                        if not last:
                            pe.wait_ge(s["v_copied"], 2 * (g + 2))
                        task_logits(g - 1)
                    if b == 7 and not first:
                        task_ranks(g - 1)
                    transpose_probs(n, b, first)
                    if b == 0:
                        if not first:
                            heads(n - 1, BG - 1, 1 - par, None)
                    else:
                        quads = None if (b - 1) % 4 or (first and b == 1) else 2 * g + (b - 1) // 4
                        heads(n - 1, b - 1, par, quads)

            groups(pe, body)
            heads(BG * GROUPS - 1, BG - 1, 1, None)
            g = GROUPS - 1
            pe.wait_ge(s["place_step"], PLACE_STEPS * g)
            task_attn(g, 1)
            pe.wait_ge(s["res_done"], g + 1)
            task_x2T(g, 1)
            pe.wait_ge(s["route_step"], ROUTE_STEPS * g)
            task_logits(g)
            task_ranks(g)

            def slots_T(e, par, half, i):
                for j in range(4 * i, min(4 * i + 4, J)):
                    last = nc.tensor.transpose(bank[4 + i % 2][:, (j - 4 * i) * P:(j - 4 * i + 1) * P], xs[par][:, j, 0:D], ident[:, :])
                last.then_inc(s["xsT_done"], 1)

            def expert(e, half, par):
                pe.wait_ge(xs_loaded[par], 16 * (half + 1))
                for i in range(3):
                    if i < 2:
                        wait_later(pe, s["xsT_copied"], 3 * e)
                    else:
                        pe.wait_ge(s["xsT_copied"], 3 * e + 1)
                    slots_T(e, par, half, i)
                pe.wait_ge(fc_loaded[par], 16 * (half + 1))
                for c in range(HC):
                    for i, (a, b) in enumerate(((0, 512), (512, 1024), (1024, CAP))):
                        if c == 0:
                            pe.wait_ge(s["xsT_copied"], 3 * e + i + 1)
                        u = 3 * c + i
                        if u >= 4:
                            pe.wait_ge(s["gelu_done"], 3 * HC * e + u - 3)
                        mm(bank[u % 4][:, 0:b - a], fc_s[par][:, c * P:(c + 1) * P], xsT[:, a:b], start=True, stop=True).then_inc(s["up_done"], 1)
                pe.wait_ge(pj_loaded[par], 16 * (half + 1))
                for j in range(J):
                    if j % 4 == 0 and j:
                        pe.wait_ge(s["gelu_done"], 3 * HC * (e + 1) - 2 + min(j // 4, 2))
                    elif j == 0:
                        pe.wait_ge(s["gelu_done"], 3 * HC * (e + 1) - 2)
                    if j == 8:
                        pe.wait_ge(s["y_step"], 3 * e + 1)
                    for c in range(HC):
                        last = mm(bank[6 + (j // 4) % 2][:, (j % 4) * D:(j % 4 + 1) * D], hT[:, c, j * P:(j + 1) * P], pj_s[par][:, c, :],
                                  start=c == 0, stop=c == HC - 1)
                    last.then_inc(s["down_done"], 1)

            experts(pe, expert)


_INS = ["x", "ctx_1024", "mask_BxS2_ff1", "L0_xattn_Wq", "L0_xattn_bq", "L0_xattn_Wk", "L0_xattn_bk", "L0_xattn_Wv",
        "L0_xattn_bv", "L0_xattn_Wo", "L0_xattn_bo", "L0_ffn_gate_w", "L0_ffn_c_fc", "L0_ffn_fc_bias",
        "L0_ffn_c_proj", "L0_ffn_proj_bias"]


def kernel(**inputs):
    import concourse.bacc as bacc
    from concourse.bass_utils import run_bass_kernel_spmd

    nc = bacc.Bacc("TRN2", target_bir_lowering=False, num_devices=1)
    arrays, args = {}, []
    for name in _INS:
        a = np.ascontiguousarray(inputs[name])
        if name == "L0_ffn_fc_bias":
            e, _, h = a.shape
            a = np.ascontiguousarray(a.reshape(e * (h // P), P).T)
        arrays[f"in_{name}"] = a
        args.append(nc.dram_tensor(f"in_{name}", a.shape, mybir.dt.from_np(a.dtype), kind="ExternalInput").ap())
    shape = inputs["x"].shape
    args.append(nc.dram_tensor("out_x", shape, F32, kind="ExternalOutput").ap())
    xattn_moe(nc, *args)
    r = run_bass_kernel_spmd(nc, [arrays], core_ids=[0])
    return r.results[0]["out_x"]
```

```python
from contextlib import ExitStack

import concourse.bass as bass
import numpy as np
from concourse import mybir

F32 = mybir.dt.float32
BF16 = mybir.dt.bfloat16
I32 = mybir.dt.int32
U32 = mybir.dt.uint32
ALU = mybir.AluOpType
ACT = mybir.ActivationFunctionType
AX = mybir.AxisListType

P = 128
TG = 4
NOWHERE = 1.0e6
EPS = 1e-5


def wait_before(engine, sem, value, met):
    if not isinstance(value, int):
        value = engine.compute_val(value)
    engine.wait_ge(met, 1)
    engine.wait_ge(sem, value)


def wait_later(engine, sem, value):
    if not isinstance(value, int) or value > 0:
        engine.wait_ge(sem, value)


class Chain:

    def __init__(self, engine, sem, per, turn):
        self.engine, self.sem, self.per, self.base, self.k = engine, sem, per, turn * per, 0

    def step(self, instruction):
        self.k += 1
        instruction.then_inc(self.sem, 1)
        self.engine.wait_ge(self.sem, self.base + self.k)

    def mark(self, instruction):
        self.k += 1
        instruction.then_inc(self.sem, 1)

    def end(self):
        assert self.k == self.per, (self.k, self.per)


def xattn_moe(nc, x, ctx_in, mask, wq, bq, wk, bk, wv, bv, wo, bo, gate_w, c_fc, fc_bias, c_proj, proj_bias, out):
    B, S, D = x.shape
    E, _, HID = c_fc.shape
    N = B * S
    H, DH = 16, D // 16
    PAIRS = H // 2
    GROUPS = N // (TG * P)
    TILES = N // P
    BG = TG * P // S
    TOK = TG * P
    CAP = int(1.25 * N * 2 / E)
    J = CAP // P
    HC = HID // P
    LINE = 2 * N
    ROW = D + 3
    SCALE = float(np.float32(1.0) / np.sqrt(np.float32(DH)))
    LOOPS = (GROUPS - 2) // 2
    assert S == 64 and D == P and CAP == J * P and GROUPS % 2 == 0 and E == 8

    x_v = x.rearrange("b s d -> (b s) d").rearrange("(t p) d -> p t d", p=P)
    ctx_v = ctx_in.rearrange("b s d -> (b s) d").rearrange("(t p) d -> p t d", p=P)
    out_v = out.rearrange("b s d -> (b s) d").rearrange("(t p) d -> p t d", p=P)
    lines = nc.dram_tensor("lines", [E * LINE, ROW], F32, kind="Internal").ap()
    lines_fill = lines.rearrange("(e l) r -> e l r", e=E)[:, N:N + CAP, :].rearrange("e (p j) r -> p e (j r)", p=P)
    out_rows = out.rearrange("b s d -> (b s) d")

    with ExitStack() as stack:
        def sb(name, shape, dt=F32):
            return stack.enter_context(nc.sbuf_tensor(name, shape, dt))

        def sem(name):
            return stack.enter_context(nc.semaphore(name))

        bank = [stack.enter_context(nc.psum_tensor(f"bank{i}", [P, 512], F32)) for i in range(8)]
        score_bank, pt_bank, r_bank, o_bank, misc_a, misc_b = bank[0:2], bank[2], bank[3], bank[4:6], bank[6], bank[7]

        ident = sb("ident", [P, P])
        mask_rows = sb("mask_rows", [P, B, S], BF16)
        three_ones = sb("three_ones", [P, P], BF16)
        before = sb("before", [P, P], BF16)
        all_ones = sb("all_ones", [P, P], BF16)
        iota8 = sb("iota8", [P, E])
        sign = sb("sign", [P, 2, E])
        number = sb("number", [P, TILES])
        slot = sb("slot", [P, J])
        middle = sb("middle", [P, E])
        next_row = sb("next_row", [P, 2, E])
        eps_t = sb("eps_t", [P, TILES])
        half_t = sb("half_t", [P, TILES])
        minus_t = sb("minus_t", [P, TG])
        w_in = sb("w_in", [P, 4, D])
        wq_s, wk_s, wv_s, wo_s = (w_in[:, i, :] for i in range(4))
        gate_s = sb("gate_s", [P, E])
        cols = sb("cols", [P, 3])
        q_scale = sb("q_scale", [P, 2])
        q_bias = sb("q_bias", [P, 2])
        bo_b = sb("bo_b", [P, D])
        out_bias = sb("out_bias", [P, D])
        mask_in = sb("mask_in", [B, S])
        mask_f = sb("mask_f", [B, 2, S])
        mask_p = sb("mask_p", [B, 3, S], BF16)
        fc_b = sb("fc_b", [P, E * HC])
        fc_e = [sb(f"fc_e{i}", [P, HC]) for i in range(2)]
        pj_b = sb("pj_b", [P, E, D])

        res = sb("res", [P, TILES, D])
        stats = sb("stats", [P, TILES, 6])
        ln = sb("ln", [P, 4, TILES])
        mean1, rstd1 = ln[:, 0, :], ln[:, 3, :]
        ctx_s = [sb(f"ctx_s{i}", [P, TG, D]) for i in range(2)]
        xn = [sb(f"xn{i}", [P, TG, D]) for i in range(2)]
        xT = sb("xT", [P, TOK])
        cT = sb("cT", [P, TOK])
        kT = sb("kT", [P, TOK])
        q_blk = [sb(f"q_blk{i}", [P, BG, 2, S]) for i in range(2)]
        k_blk = [sb(f"k_blk{i}", [P, PAIRS, TOK]) for i in range(2)]
        v_blk = [sb(f"v_blk{i}", [P, BG, TG, 2, 2 * DH]) for i in range(2)]
        top = sb("top", [P, 4, PAIRS])
        probs = [sb(f"probs{i}", [P, PAIRS, S]) for i in range(4)]
        total = sb("total", [P, 4, PAIRS])
        recip = sb("recip", [P, 4, PAIRS])
        half_rows = sb("half_rows", [P, 2, DH])
        recip_rows = [sb(f"recip_rows{i}", [P, PAIRS, 2, DH]) for i in range(2)]
        pT = [sb(f"pT{i}", [P, 512]) for i in range(2)]
        rT = sb("rT", [P, 512])
        o_mul = sb("o_mul", [P, 4, 2, S])
        oT = [sb(f"oT{i}", [P, TOK]) for i in range(2)]

        row = [sb(f"row{i}", [P, TG, ROW]) for i in range(2)]
        rows_at = [sb(f"rows_at{i}", [P, TG, 2], I32) for i in range(2)]
        stats2 = sb("stats2", [P, TG, 6])
        aggr2 = sb("aggr2", [P, TG, 2])
        rstd2 = sb("rstd2", [P, 4, TG])
        x2T = sb("x2T", [P, TOK])
        logits = sb("logits", [P, TG, E])
        best = sb("best", [P, TG, 8])
        best_at = sb("best_at", [P, TG, 8], U32)
        chosen = sb("chosen", [P, TG, 2, E], BF16)
        signed = sb("signed", [P, TG, 2, E], BF16)
        gap = sb("gap", [P, 3, TG])
        place = sb("place", [P, TG, 2, E])
        place_f = sb("place_f", [P, TG, 2])

        start_i = sb("start_i", [P, E], I32)
        n_first = sb("n_first", [P, E])
        n_all = sb("n_all", [P, E])
        first_f = sb("first_f", [P, E])
        xs = [sb(f"xs{i}", [P, J, ROW]) for i in range(2)]
        fc_s = [sb(f"fc_s{i}", [P, HID]) for i in range(2)]
        pj_s = [sb(f"pj_s{i}", [P, HC, D]) for i in range(2)]
        xsT = sb("xsT", [P, CAP])
        hT = sb("hT", [P, HC, CAP])
        y_s = [k_blk[0][:, 0:3, :].rearrange("p a b -> p (a b)")[:, 0:CAP].rearrange("p (j d) -> p j d", d=D),
               k_blk[0][:, 4:7, :].rearrange("p a b -> p (a b)")[:, 0:CAP].rearrange("p (j d) -> p j d", d=D)]
        y_at = [sb(f"y_at{i}", [P, J], I32) for i in range(2)]
        slot_w = [sb(f"slot_w{i}", [P, J]) for i in range(2)]
        slot_t = sb("slot_t", [P, 4, J])
        fill = xs[0]

        names = """w_loaded small_loaded x_loaded0 x_loaded ctx_loaded0 ctx_loaded1 k_placed0 k_placed1 mask_placed stats_done ones_made
            consts_made fill_made filled setup v_bias_done out_bias_done heads_made inverted ln1_step rstd1_half rstd1_done rstd2_half centred
            xn_done xT_done cT_done k_done q_done v_done attn_done x2T_done logits_done ranks_done bias_done ffn_loaded keys_cleared0 keys_cleared1 values_cleared
            xT_copied cT_copied k_copied q_copied v_copied x2T_copied biased
            scores_done top_done shifted exp_done sum_step recip_done probsT_done probsT_copied
            heads_done recipT_copied o_step res_done ln2_step rstd2_done row_done
            route_step chosen_done gap_exp place_step scattered0 scattered1
            window_step start_done xs_loaded0 xs_loaded1 fc_loaded0 fc_loaded1 pj_loaded0 pj_loaded1
            xsT_done xsT_copied up_done gelu_done down_done slot_step y_done y_step y_scattered0 y_scattered1
            stored""".split()
        s = {n: sem(n) for n in names}
        x_loaded0, ln1_step = s["x_loaded0"], s["ln1_step"]
        ctx_loaded, k_placed = [s["ctx_loaded0"], s["ctx_loaded1"]], [s["k_placed0"], s["k_placed1"]]
        scattered, xs_loaded = [s["scattered0"], s["scattered1"]], [s["xs_loaded0"], s["xs_loaded1"]]
        fc_loaded, pj_loaded = [s["fc_loaded0"], s["fc_loaded1"]], [s["pj_loaded0"], s["pj_loaded1"]]
        y_scattered = [s["y_scattered0"], s["y_scattered1"]]

        AHEAD = 2
        LN1_STEPS, LN2_STEPS, ROUTE_STEPS, PLACE_STEPS, WINDOW_STEPS, SLOT_STEPS = 7, 8, 11, 7, 6, 6

        MIDDLE = dict(logits=0, choose=1, exp_gap=2, cT=0, xT=1, k=1, q=2, join1=2, attn=3, v=4, residual=5, ranks=5,
                      place=6, join0=6, normalise2=6, x2T=7)
        LAST = dict(logits=0, choose=1, exp_gap=2, ranks=1, place=2, join1=1, attn=2, residual=4, normalise2=5, x2T=5,
                    join0=6, logits1=6, choose1=7, ranks1=7)

        def groups(engine, body):
            body(0, 0, 0, True, False)
            body(1, 0, 1, False, False)
            with engine.Fori(1, GROUPS // 2 - 1) as i:
                body(2 * i, i, 0, False, False)
                body(2 * i + 1, i, 1, False, False)
            body(GROUPS - 2, GROUPS // 2 - 1, 0, False, False)
            body(GROUPS - 1, GROUPS // 2 - 1, 1, False, True)

        def experts(engine, body):
            body(0, 0, 0)
            body(1, 0, 1)
            with engine.Fori(1, E // 2) as i:
                body(2 * i, i, 0)
                body(2 * i + 1, i, 1)

        block = stack.enter_context(nc.Block())

        @block.sync
        def _(sp):
            def load_ctx(g, par):
                sp.dma_start(ctx_s[par][:, :, :], ctx_v[:, bass.ds(g * TG, TG), :]).then_inc(ctx_loaded[par], 16)

            def store_residual(g):
                wait_before(sp, s["res_done"], g + 1, s["consts_made"])
                sp.dma_start(out_v[:, bass.ds(g * TG, TG), :], res[:, bass.ds(g * TG, TG), :]).then_inc(s["stored"], 16)

            def place_keys(g, par):
                wait_before(sp, s["k_copied"], g + 1, s["consts_made"])
                for pair in range(PAIRS):
                    r = slice(2 * DH * pair, 2 * DH * (pair + 1))
                    sp.dma_start(k_blk[par][r, pair, :], kT[r, :]).then_inc(k_placed[par], 16)

            sp.dma_start(res[:, 0:TG, :], x_v[:, 0:TG, :]).then_inc(x_loaded0, 16)
            load_ctx(0, 0)
            for i, w in enumerate((wq, wk, wv, wo)):
                sp.dma_start(w_in[:, i, :], w).then_inc(s["w_loaded"], 16)
            sp.dma_start(res[:, TG:TILES, :], x_v[:, TG:TILES, :]).then_inc(s["x_loaded"], 16)
            load_ctx(1, 1)
            sp.dma_start(fc_b[:, :], fc_bias).then_inc(s["ffn_loaded"], 16)
            sp.dma_start(pj_b[:, :, :], proj_bias.rearrange("e a d -> a e d").to_broadcast([P, E, D])).then_inc(s["ffn_loaded"], 16)
            sp.wait_ge(s["setup"], 4)
            sp.wait_ge(s["consts_made"], 1)
            for i in range(3):
                sp.dma_start(mask_rows[i:i + 1, :, :], mask_p[:, i, :]).then_inc(s["mask_placed"], 16)
            sp.wait_ge(s["keys_cleared0"], 1)
            place_keys(0, 0)

            def body(g, half, par, first, last):
                if not (last or first):
                    wait_before(sp, s["cT_done"], g, s["consts_made"])
                    load_ctx(g + 1, 1 - par)
                if not last:
                    if not first:
                        wait_before(sp, s["scores_done"], BG * g, s["consts_made"])
                    place_keys(g + 1, 1 - par)
                if not first:
                    store_residual(g - 1)

            groups(sp, body)
            store_residual(GROUPS - 1)

            def load_weights(e, par):
                sp.dma_start(fc_s[par][:, :], c_fc.rearrange("e d h -> d e h")[:, bass.ds(e, 1), :].rearrange("d e h -> d (e h)")
                             ).then_inc(fc_loaded[par], 16)
                sp.dma_start(pj_s[par][:, :, :], c_proj.rearrange("e (c p) d -> p e c d", p=P)[:, bass.ds(e, 1), :, :]
                             .rearrange("p e c d -> p (e c) d")).then_inc(pj_loaded[par], 16)

            def window_start(e):
                return sp.value_load(start_i[0:1, bass.ds(e, 1)], min_val=0, max_val=E * LINE - CAP)

            def load_window(par, start):
                sp.dma_start(xs[par][:, :, :].rearrange("p j r -> p (j r)"),
                             lines[bass.ds(start, CAP), :].rearrange("(p j) r -> p (j r)", p=P)).then_inc(xs_loaded[par], 16)

            load_weights(0, 0)
            load_weights(1, 1)
            sp.wait_ge(s["start_done"], 1)
            starts = [window_start(e) for e in range(2)]
            for par in range(2):
                sp.wait_ge(scattered[par], 16 * 2 * TG * GROUPS // 2)
            for par in range(2):
                load_window(par, starts[par])
            with sp.Fori(0, E // 2 - 1) as i:
                for par in range(2):
                    e = 2 * i + par
                    wait_before(sp, s["down_done"], J * (e + 1), s["consts_made"])
                    load_weights(e + 2, par)
                    wait_before(sp, s["slot_step"], SLOT_STEPS * (e + 1), s["consts_made"])
                    wait_before(sp, s["xsT_done"], 3 * (e + 1), s["consts_made"])
                    load_window(par, window_start(e + 2))

            sp.wait_ge(s["stored"], 16 * GROUPS)

        @block.gpsimd
        def _(pool):
            pool.memset(ident[:, :], 0.0).then_inc(s["consts_made"], 1)
            pool.memset(before[:, :], 1.0).then_inc(s["consts_made"], 1)
            pool.wait_ge(s["consts_made"], 2)
            pool.affine_select(out=ident[:, :], in_=ident[:, :], compare_op=ALU.not_equal, fill=1.0, base=0,
                               pattern=[[-1, P]], channel_multiplier=1).then_inc(s["consts_made"], 1)
            pool.affine_select(out=before[:, :], in_=before[:, :], compare_op=ALU.is_gt, fill=0.0, base=0,
                               pattern=[[1, P]], channel_multiplier=-1).then_inc(s["consts_made"], 1)
            pool.memset(eps_t[:, :], EPS)
            pool.memset(minus_t[:, :], -1.0)
            pool.memset(half_t[:, :], -0.5).then_inc(s["consts_made"], 1)
            pool.wait_ge(s["consts_made"], 5)

            def rstd(variance, half, out_, n, gate, done):
                pool.tensor_tensor(half, variance, eps_t[:, 0:n], ALU.add).then_inc(s["rstd1_half"], 1)
                pool.wait_ge(s["rstd1_half"], gate)
                pool.tensor_tensor(out_, half, half_t[:, 0:n], ALU.pow).then_inc(done, 1)

            def normalise1(g, par, loop=True):
                wait_later(pool, s["xT_done"], g - 1)
                x_g = res[:, bass.ds(g * TG, TG), :]
                m, q = (a[:, bass.ds(g * TG, TG)].rearrange("p (t b) -> p t b", b=1).to_broadcast([P, TG, D]) for a in (mean1, rstd1))
                pool.tensor_tensor(xn[par][:, :, :], x_g, m, ALU.subtract).then_inc(s["centred"], 1)
                pool.wait_ge(s["centred"], g)
                pool.tensor_tensor(xn[par][:, :, :], xn[par][:, :, :], q, ALU.mult).then_inc(s["xn_done"], 1)

            def bias_residual(g, read=False):
                if not read:
                    wait_before(pool, s["centred"], g, s["consts_made"])
                r = res[:, bass.ds(g * TG, TG), :]
                pool.tensor_tensor(r, r, out_bias[:, :].rearrange("p (a d) -> p a d", a=1).to_broadcast([P, TG, D]), ALU.add).then_inc(s["biased"], 1)

            pool.wait_ge(ln1_step, LN1_STEPS)
            rstd(ln[:, 1, 0:TG], ln[:, 2, 0:TG], ln[:, 3, 0:TG], TG, 1, s["rstd1_done"])
            for i in range(2):
                pool.memset(v_blk[i][:, :, :, :, :], 0.0).then_inc(s["values_cleared"], 1)
            pool.iota(iota8[:, :], pattern=[[1, E]], base=0, channel_multiplier=0, allow_small_or_imprecise_dtypes=True)
            pool.iota(next_row[:, :, :], pattern=[[1, 2], [LINE, E]], base=N - 1, channel_multiplier=0, allow_small_or_imprecise_dtypes=True)
            pool.iota(middle[:, :], pattern=[[LINE, E]], base=N, channel_multiplier=0, allow_small_or_imprecise_dtypes=True)
            pool.iota(number[:, :], pattern=[[P, TILES]], base=0, channel_multiplier=1, allow_small_or_imprecise_dtypes=True)
            pool.iota(slot[:, :], pattern=[[1, J]], base=0, channel_multiplier=J, allow_small_or_imprecise_dtypes=True)
            pool.memset(all_ones[:, :], 1.0)
            pool.memset(sign[:, 0, :], -1.0)
            pool.memset(sign[:, 1, :], 1.0).then_inc(s["consts_made"], 1)
            pool.memset(k_blk[1][:, :, :], 0.0).then_inc(s["keys_cleared1"], 1)
            pool.memset(fill[:, :, :], 0.0).then_inc(s["fill_made"], 1)
            pool.wait_ge(s["fill_made"], 1)
            pool.memset(fill[:, :, D + 2:D + 3], NOWHERE).then_inc(s["fill_made"], 1)
            pool.wait_ge(ln1_step, 2 * LN1_STEPS)
            rstd(ln[:, 1, TG:TILES], ln[:, 2, TG:TILES], ln[:, 3, TG:TILES], TILES - TG, 2, s["rstd1_done"])
            pool.wait_ge(s["rstd1_done"], 2)
            normalise1(1, 1)
            pool.wait_ge(s["fill_made"], 2)
            for e in range(E):
                pool.dma_start(lines_fill[:, e, :], fill[:, :, :].rearrange("p j r -> p (j r)")).then_inc(s["filled"], 16)
            def route(g, half, par, tiles=range(TG)):
                wait_before(pool, s["place_step"], PLACE_STEPS * (g + 1), s["consts_made"])
                for t in tiles:
                    for k in range(2):
                        pool.indirect_dma_start(
                            lines, bass.IndirectOffsetOnAxis(ap=rows_at[par][:, t, k:k + 1], axis=0), row[par][:, t, :], None,
                            bounds_check=E * LINE - 1, oob_is_err=False).then_inc(scattered[par], 16)

            def power2(g):
                pool.wait_ge(s["ln2_step"], LN2_STEPS * (g + 1))
                wait_later(pool, s["row_done"], g)
                pool.tensor_tensor(rstd2[:, 2, :], aggr2[:, :, 0], minus_t[:, :], ALU.mult)
                rstd(aggr2[:, :, 1], rstd2[:, 0, :], rstd2[:, 1, :], TG, g + 3, s["rstd2_half"])
                pool.wait_ge(s["rstd2_half"], g + 1)
                pool.tensor_tensor(rstd2[:, 3, :], rstd2[:, 1, :], rstd2[:, 2, :], ALU.mult).then_inc(s["rstd2_done"], 1)

            pool.wait_ge(s["out_bias_done"], 2)
            pool.wait_ge(s["xn_done"], 1)
            bias_residual(0, True)
            bias_residual(1)

            def body(g, half, par, first, last):
                if not (isinstance(g, int) and g + 2 >= GROUPS):
                    normalise1(g + 2, par)
                    bias_residual(g + 2)
                if isinstance(g, int) and g == 1:
                    pool.wait_ge(s["filled"], 16 * E)
                if last:
                    route(g - 2, half - 1, par)
                if not first:
                    power2(g - 1)
                if not (last or isinstance(g, int) and g < 2):
                    route(g - 2, half - 1, par)

            groups(pool, body)
            route(GROUPS - 2, 0, 0, range(0, TG // 2))
            power2(GROUPS - 1)
            route(GROUPS - 2, 0, 0, range(TG // 2, TG))
            route(GROUPS - 1, 0, 1)

            def scatter(e, half, par):
                pool.wait_ge(s["slot_step"], SLOT_STEPS * (e + 1))
                wait_later(pool, y_scattered[1 - par], 16 * J * (half + par))
                for j in range(J):
                    if j % 4 == 0:
                        wait_before(pool, s["y_done"], 3 * e + j // 4 + 1, s["consts_made"])
                    pool.indirect_dma_start(
                        out_rows, bass.IndirectOffsetOnAxis(ap=y_at[par][:, j:j + 1], axis=0), y_s[par][:, j, :], None,
                        bounds_check=N - 1, oob_is_err=False, compute_op=ALU.add).then_inc(y_scattered[par], 16)

            pool.wait_ge(s["stored"], 16 * GROUPS)
            experts(pool, scatter)
            for par in range(2):
                pool.wait_ge(y_scattered[par], 16 * J * E // 2)

        @block.scalar
        def _(act):
            for i, b_ in enumerate((bq, bk, bv)):
                act.dma_start(cols[:, i:i + 1], b_.rearrange("(p a) -> p a", a=1)).then_inc(s["small_loaded"], 16)
            act.dma_start(mask_in[:, :], mask).then_inc(s["small_loaded"], 16)
            act.dma_start(bo_b[:, :], bo.rearrange("(a d) -> a d", a=1).to_broadcast([P, D])).then_inc(s["small_loaded"], 16)
            act.dma_start(gate_s[:, :], gate_w).then_inc(s["small_loaded"], 16)

            def copy(dst, src, done, **bias):
                act.activation(dst, src, ACT.Identity, **bias).then_inc(done, 1)

            def copy_cT(g):
                act.wait_ge(s["cT_done"], g + 1)
                wait_later(act, s["v_done"], g)
                copy(cT[:, :], misc_a[:, :], s["cT_copied"])

            def copy_xT(g):
                act.wait_ge(s["xT_done"], g + 1)
                wait_later(act, s["q_done"], g)
                copy(xT[:, :], misc_b[:, :], s["xT_copied"])

            def copy_k(g, half, par):
                act.wait_ge(s["k_done"], g + 1)
                wait_later(act, k_placed[1 - par], 16 * PAIRS * (half if par == 0 else half + 1))
                copy(kT[:, :], misc_a[:, :], s["k_copied"], bias=cols[:, 1:2])

            def copy_q(g, par):
                act.wait_ge(s["q_done"], g + 1)
                for h2 in range(2):
                    copy(q_blk[par][:, :, h2, :], misc_a[:, :].rearrange("p (b q) -> p b q", b=BG), s["q_copied"],
                         bias=q_bias[:, h2:h2 + 1], scale=q_scale[:, h2:h2 + 1])

            def copy_v(g, par):
                act.wait_ge(s["v_done"], g + 1)
                for pp in range(2):
                    r = slice(S * pp, S * (pp + 1))
                    copy(v_blk[par][r, :, :, pp, :].rearrange("k b j c -> k (b j) c"),
                         misc_a[r, :].rearrange("k (a c) -> k a c", c=2 * DH), s["v_copied"])

            def exp(n, k):
                act.wait_ge(s["shifted"], n + 1)
                act.activation(probs[k % 4][:, :, :], probs[k % 4][:, :, :], ACT.Exp).then_inc(s["exp_done"], 1)

            def copy_probsT(n, b, first):
                act.wait_ge(s["probsT_done"], n + 1)
                if not (first and b < 2):
                    act.wait_ge(s["heads_done"], n - 1)
                copy(pT[b % 2][:, :], pt_bank[:, :], s["probsT_copied"])

            def copy_recipT(quad, first):
                act.wait_ge(s["heads_done"], 4 * (quad + 1))
                if not first:
                    act.wait_ge(s["o_step"], 2 * quad)
                copy(rT[:, :], r_bank[:, :], s["recipT_copied"])

            def copy_x2T(g):
                act.wait_ge(s["x2T_done"], g + 1)
                wait_later(act, s["logits_done"], g)
                copy(x2T[:, :], misc_a[:, :], s["x2T_copied"])

            def normalise2(g, half, par):
                act.wait_ge(s["rstd2_done"], g + 1)
                wait_later(act, scattered[par], 16 * 2 * TG * half)
                for t in range(TG):
                    last = act.activation(row[par][:, t, 0:D], res[:, bass.ds(g * TG + t, 1), :].rearrange("p a d -> p (a d)"),
                                          ACT.Identity, bias=rstd2[:, 3, t:t + 1], scale=rstd2[:, 1, t:t + 1])
                last.then_inc(s["row_done"], 1)

            def exp_gap(g):
                act.wait_ge(s["chosen_done"], g + 1)
                act.activation(gap[:, 1, :], gap[:, 0, :], ACT.Exp).then_inc(s["gap_exp"], 1)

            copy_xT(0)
            copy_cT(0)
            act.wait_ge(s["small_loaded"], 16 * 6)
            copy_k(0, 0, 0)
            act.wait_ge(s["setup"], 3)
            copy_q(0, 0)
            act.wait_ge(s["values_cleared"], 2)
            copy_v(0, 0)
            for n in range(AHEAD):
                exp(n, n)

            def body(g, half, par, first, last):
                for b in range(BG):
                    n = BG * g + b
                    at = LAST if last else MIDDLE
                    copy_probsT(n, b, first)
                    if b == 1 and not first:
                        copy_recipT(2 * g - 1, False)
                    if b == 5:
                        copy_recipT(2 * g, first)
                    if b == at["exp_gap"] and not (isinstance(g, int) and g < 2):
                        exp_gap(g - 2)
                    if not (last and b >= BG - AHEAD):
                        exp(n + AHEAD, b + AHEAD)
                    if not last:
                        if b == at["cT"]:
                            copy_cT(g + 1)
                        if b == at["xT"]:
                            copy_xT(g + 1)
                        if b == at["k"]:
                            copy_k(g + 1, half if par == 0 else half + 1, 1 - par)
                        if b == at["q"]:
                            copy_q(g + 1, 1 - par)
                        if b == at["v"]:
                            copy_v(g + 1, 1 - par)
                    if not first:
                        if b == at["normalise2"]:
                            normalise2(g - 1, half if par == 1 else half - 1, 1 - par)
                        if b == at["x2T"]:
                            copy_x2T(g - 1)

            groups(act, body)
            exp_gap(GROUPS - 2)
            copy_recipT(2 * GROUPS - 1, False)
            normalise2(GROUPS - 1, GROUPS // 2 - 1, 1)
            copy_x2T(GROUPS - 1)
            exp_gap(GROUPS - 1)

            def gelus(e, half, par):
                act.wait_ge(s["bias_done"], e + 1)
                for c in range(HC):
                    for i, (a, b) in enumerate(((0, 512), (512, 1024), (1024, CAP))):
                        act.wait_ge(s["up_done"], 3 * HC * e + 3 * c + i + 1)
                        act.activation(hT[:, c, a:b], bank[(3 * c + i) % 4][:, 0:b - a], ACT.Gelu,
                                       bias=fc_e[par][:, c:c + 1]).then_inc(s["gelu_done"], 1)

            experts(act, gelus)

        @block.vector
        def _(dve):
            v = nc.vector
            v.memset(mask_rows[:, :, :], 0.0).then_inc(s["setup"], 1)

            def ln1(t0, t1, turn):
                ch = Chain(dve, ln1_step, LN1_STEPS, turn)
                m, var, tmp = ln[:, 0, t0:t1], ln[:, 1, t0:t1], ln[:, 2, t0:t1]
                st = stats[:, t0:t1, :]
                ch.step(v.tensor_tensor(m, st[:, :, 1], st[:, :, 4], ALU.add))
                ch.step(v.tensor_scalar(m, m, 0.5, None, ALU.mult))
                ch.step(v.tensor_tensor(tmp, st[:, :, 1], m, ALU.subtract))
                ch.step(v.tensor_tensor(tmp, tmp, tmp, ALU.mult))
                ch.step(v.tensor_tensor(var, st[:, :, 2], st[:, :, 5], ALU.add))
                ch.step(v.tensor_scalar(var, var, 1.0 / D, None, ALU.mult))
                ch.step(v.tensor_tensor(var, var, tmp, ALU.add))
                ch.end()

            dve.wait_ge(x_loaded0, 16)
            for t in range(TG):
                v.bn_stats(stats[:, t, :], res[:, t, :]).then_inc(s["stats_done"], 1)
            dve.wait_ge(s["stats_done"], TG)
            ln1(0, TG, 0)
            v.memset(k_blk[0][:, 0:2, :], 0.0)
            dve.wait_ge(s["rstd1_done"], 1)
            for t in range(TG):
                last = v.tensor_scalar(xn[0][:, t, :], res[:, t, :], mean1[:, t:t + 1], rstd1[:, t:t + 1], ALU.subtract, ALU.mult)
            last.then_inc(s["xn_done"], 1)
            v.memset(k_blk[0][:, 2:PAIRS, :], 0.0).then_inc(s["keys_cleared0"], 1)
            dve.wait_ge(s["consts_made"], 5)
            v.reduce_sum(q_scale[:, :], ident[:, :].rearrange("p (a h d) -> p h a d", h=2, d=DH), AX.XY).then_inc(s["out_bias_done"], 1)
            dve.wait_ge(s["out_bias_done"], 1)
            v.tensor_scalar(q_scale[:, :], q_scale[:, :], SCALE, None, ALU.mult).then_inc(s["setup"], 1)
            dve.wait_ge(s["setup"], 2)
            dve.wait_ge(s["small_loaded"], 16 * 6)
            v.tensor_scalar(q_bias[:, :], q_scale[:, :], cols[:, 0:1], None, ALU.mult).then_inc(s["setup"], 1)
            mch = Chain(dve, s["window_step"], 6, 0)
            mch.step(v.tensor_scalar(mask_f[:, 0, :], mask_in[:, :], -1.0, 1.0, ALU.mult, ALU.add))
            mch.step(v.tensor_scalar(mask_f[:, 0, :], mask_f[:, 0, :], -1.0e30, None, ALU.mult))
            mch.step(v.tensor_copy(mask_p[:, 0, :], mask_f[:, 0, :]))
            mch.step(v.tensor_tensor(mask_f[:, 1, :], mask_f[:, 0, :], mask_p[:, 0, :], ALU.subtract))
            mch.step(v.tensor_copy(mask_p[:, 1, :], mask_f[:, 1, :]))
            mch.step(v.tensor_tensor(mask_f[:, 0, :], mask_f[:, 1, :], mask_p[:, 1, :], ALU.subtract))
            v.tensor_copy(mask_p[:, 2, :], mask_f[:, 0, :]).then_inc(s["setup"], 1)
            v.memset(three_ones[:, :], 0.0).then_inc(s["ones_made"], 1)
            dve.wait_ge(s["ones_made"], 1)
            v.memset(three_ones[0:3, :], 1.0).then_inc(s["ones_made"], 1)
            v.memset(half_rows[:, :, :], 0.0).then_inc(s["heads_made"], 1)
            dve.wait_ge(s["heads_made"], 1)
            for h2 in range(2):
                v.memset(half_rows[S * h2:S * (h2 + 1), h2, :], 1.0).then_inc(s["heads_made"], 1)
            dve.wait_ge(s["heads_made"], 3)
            dve.wait_ge(s["x_loaded"], 16)
            for t in range(TG, TILES):
                v.bn_stats(stats[:, t, :], res[:, t, :]).then_inc(s["stats_done"], 1)
            dve.wait_ge(s["stats_done"], TILES)
            ln1(TG, TILES, 1)
            dve.wait_ge(s["attn_done"], 1)
            v.tensor_tensor(out_bias[:, :], misc_b[:, 0:D], bo_b[:, :], ALU.add).then_inc(s["out_bias_done"], 1)

            def top_of(n, k):
                dve.wait_ge(s["scores_done"], n + 1)
                sc = score_bank[k % 2][:, :].rearrange("p (a k) -> p a k", k=S)
                v.reduce_max(top[:, k % 4, :], sc, AX.X).then_inc(s["top_done"], 1)

            def shift(n, k):
                sc = score_bank[k % 2][:, :].rearrange("p (a k) -> p a k", k=S)
                wait_later(dve, s["probsT_done"], n - 3)
                dve.wait_ge(s["top_done"], n + 1)
                v.tensor_tensor(probs[k % 4][:, :, :], sc,
                                top[:, k % 4, :].rearrange("p (a b) -> p a b", b=1).to_broadcast([P, PAIRS, S]),
                                ALU.subtract).then_inc(s["shifted"], 1)

            def sums(n, k):
                dve.wait_ge(s["exp_done"], n + 1)
                v.reduce_sum(total[:, k % 4, :], probs[k % 4][:, :, :], AX.X).then_inc(s["sum_step"], 1)

            def invert(n, k):
                dve.wait_ge(s["sum_step"], n + 1)
                v.reciprocal(recip[:, k % 4, :], total[:, k % 4, :]).then_inc(s["inverted"], 1)

            def spread(n, k):
                wait_later(dve, s["heads_done"], n - 1)
                dve.wait_ge(s["inverted"], n + 1)
                v.tensor_tensor(recip_rows[k % 2][:, :, :, :].rearrange("p a h c -> p a (h c)"),
                                recip[:, k % 4, :].rearrange("p (a b) -> p a b", b=1).to_broadcast([P, PAIRS, 2 * DH]),
                                half_rows[:, :, :].rearrange("p (b h) c -> p b (h c)", b=1).to_broadcast([P, PAIRS, 2 * DH]),
                                ALU.mult).then_inc(s["recip_done"], 1)

            def join_heads(quad, par, q2):
                dve.wait_ge(s["recipT_copied"], quad + 1)
                v.tensor_tensor(o_mul[:, :, :, :].rearrange("p b h q -> p (b h q)"), o_bank[q2][:, :], rT[:, :], ALU.mult).then_inc(s["o_step"], 1)
                dve.wait_ge(s["o_step"], 2 * quad + 1)
                v.tensor_tensor(oT[par][:, q2 * 256:(q2 + 1) * 256].rearrange("p (b q) -> p b q", b=4),
                                o_mul[:, :, 0, :], o_mul[:, :, 1, :], ALU.add).then_inc(s["o_step"], 1)

            def residual(g):
                dve.wait_ge(s["attn_done"], g + 2)
                dve.wait_ge(s["biased"], g + 1)
                r = res[:, bass.ds(g * TG, TG), :]
                v.tensor_tensor(r, misc_b[:, :].rearrange("p (t d) -> p t d", t=TG), r, ALU.add).then_inc(s["res_done"], 1)
                wait_before(dve, s["res_done"], g + 1, s["setup"])
                ch = Chain(dve, s["ln2_step"], LN2_STEPS, g)
                for t in range(TG):
                    ch.mark(v.bn_stats(stats2[:, t, :], res[:, bass.ds(g * TG + t, 1), :].rearrange("p a d -> p (a d)")))
                wait_before(dve, s["ln2_step"], ch.base + TG, s["setup"])
                for t in range(TG):
                    ch.mark(v.bn_aggr(aggr2[:, t, :], stats2[:, t, :]))
                ch.end()

            def choose(g):
                dve.wait_ge(s["logits_done"], g + 1)
                ch = Chain(dve, s["route_step"], ROUTE_STEPS, g)
                ch.mark(v.tensor_copy(logits[:, :, :].rearrange("p t e -> p (t e)"), misc_b[:, 0:TG * E]))
                wait_before(dve, s["route_step"], ch.base + 1, s["setup"])
                for t in range(TG):
                    ch.mark(v.max(best[:, t, :], logits[:, t, :]))
                wait_before(dve, s["route_step"], ch.base + 1 + TG, s["setup"])
                for t in range(TG):
                    ch.mark(v.max_index(best_at[:, t, :], best[:, t, :], logits[:, t, :]))
                dve.wait_ge(s["route_step"], ch.base + 1 + 2 * TG)
                wait_later(dve, s["ranks_done"], g)
                ch.step(v.tensor_tensor(chosen[:, :, :, :],
                                        best_at[:, :, 0:2].rearrange("p t (k a) -> p t k a", a=1).to_broadcast([P, TG, 2, E]),
                                        iota8[:, :].rearrange("p (a b e) -> p a b e", a=1, b=1).to_broadcast([P, TG, 2, E]), ALU.is_equal))
                v.tensor_tensor(gap[:, 0, :], best[:, :, 1], best[:, :, 0], ALU.subtract).then_inc(s["chosen_done"], 1)
                ch.mark(v.tensor_tensor(signed[:, :, :, :].rearrange("p t k e -> p t (k e)"), chosen[:, :, :, :].rearrange("p t k e -> p t (k e)"),
                                        sign[:, :, :].rearrange("p k e -> p (k e)").rearrange("p (a c) -> p a c", a=1).to_broadcast([P, TG, 2 * E]), ALU.mult))
                ch.end()

            def place_rows(g, half, par):
                dve.wait_ge(s["ranks_done"], g + 1)
                ch = Chain(dve, s["place_step"], PLACE_STEPS, g)
                nr = next_row[:, :, :].rearrange("p k e -> p (k e)")
                ch.step(v.tensor_tensor(place[:, :, :, :].rearrange("p t k e -> p t (k e)"),
                                        misc_b[:, 0:TG * 2 * E].rearrange("p (t c) -> p t c", t=TG),
                                        nr.rearrange("p (a c) -> p a c", a=1).to_broadcast([P, TG, 2 * E]), ALU.add))
                ch.step(v.tensor_tensor(place[:, :, :, :], place[:, :, :, :], chosen[:, :, :, :], ALU.mult))
                ch.step(v.reduce_sum(place_f[:, :, :], place[:, :, :, :], AX.X))
                v.tensor_copy(rows_at[par][:, :, :], place_f[:, :, :])
                ch.mark(v.tensor_tensor(nr, misc_b[:, TG * 2 * E:(TG + 1) * 2 * E], nr, ALU.add))
                dve.wait_ge(s["gap_exp"], g + 1)
                ch.step(v.tensor_scalar(gap[:, 2, :], gap[:, 1, :], 1.0, None, ALU.add))
                ch.step(v.reciprocal(row[par][:, :, D], gap[:, 2, :]))
                v.tensor_copy(row[par][:, :, D + 2], number[:, bass.ds(g * TG, TG)])
                ch.mark(v.tensor_tensor(row[par][:, :, D + 1], row[par][:, :, D], gap[:, 1, :], ALU.mult))
                ch.end()

            for n in range(AHEAD):
                top_of(n, n)
                shift(n, n)

            def body(g, half, par, first, last):
                for b in range(BG):
                    n = BG * g + b
                    at = LAST if last else MIDDLE
                    more = not (last and b >= BG - AHEAD)
                    late = not (isinstance(g, int) and g < 2)
                    if more:
                        top_of(n + AHEAD, b + AHEAD)
                    if not (first and b == 0):
                        spread(n - 1, b + BG - 1)
                    if b == at["residual"] and not first:
                        residual(g - 1)
                    sums(n, b)
                    if more:
                        shift(n + AHEAD, b + AHEAD)
                    invert(n, b)
                    if b == at["choose"] and late:
                        choose(g - 2)
                    if b == at["place"] and late:
                        place_rows(g - 2, half - 1, par)
                    if b == at["join1"] and not first:
                        join_heads(2 * g - 1, 1 - par, 1)
                    if b == at["join0"]:
                        join_heads(2 * g, par, 0)
                    if last and b == at["choose1"]:
                        choose(g - 1)

            groups(dve, body)
            spread(BG * GROUPS - 1, BG - 1)
            place_rows(GROUPS - 2, 0, 0)
            join_heads(2 * GROUPS - 1, 1, 1)
            residual(GROUPS - 1)
            choose(GROUPS - 1)
            place_rows(GROUPS - 1, 0, 1)

            wch = Chain(dve, s["window_step"], WINDOW_STEPS, 1)
            wch.step(v.tensor_scalar(first_f[:, :], middle[:, :], -float(CAP), None, ALU.add))
            wch.step(v.tensor_scalar(n_all[:, :], next_row[:, 0, :], 1.0, None, ALU.add))
            wch.step(v.tensor_tensor(first_f[:, :], first_f[:, :], n_all[:, :], ALU.max))
            v.tensor_copy(start_i[:, :], first_f[:, :]).then_inc(s["start_done"], 1)
            wch.step(v.tensor_tensor(n_first[:, :], middle[:, :], first_f[:, :], ALU.subtract))
            wch.step(v.tensor_tensor(n_all[:, :], next_row[:, 1, :], middle[:, :], ALU.subtract))
            wch.step(v.tensor_tensor(n_all[:, :], n_all[:, :], n_first[:, :], ALU.add))
            wch.end()

            def expert(e, half, par):
                def copy_xsT(i):
                    dve.wait_ge(s["xsT_done"], 3 * e + i + 1)
                    a, b = 512 * i, min(512 * (i + 1), CAP)
                    v.tensor_copy(xsT[:, a:b], bank[4 + i % 2][:, 0:b - a]).then_inc(s["xsT_copied"], 1)

                wait_later(dve, s["up_done"], 3 * HC * e)
                v.tensor_copy(fc_e[par][:, :], fc_b[:, bass.ds(e * HC, HC)]).then_inc(s["bias_done"], 1)
                for i in range(3):
                    copy_xsT(i)
                wait_later(dve, y_scattered[par], 16 * J * half)
                dve.wait_ge(xs_loaded[par], 16 * (half + 1))
                w0, w1, num = (xs[par][:, :, D + i] for i in range(3))
                sel, diff, none = (slot_t[:, i, :] for i in range(3))
                ch = Chain(dve, s["slot_step"], SLOT_STEPS, e)
                ch.mark(v.tensor_scalar(sel, slot[:, :], n_first[:, bass.ds(e, 1)], None, ALU.is_lt))
                ch.mark(v.tensor_scalar(none, slot[:, :], n_all[:, bass.ds(e, 1)], NOWHERE, ALU.is_ge, ALU.mult))
                ch.step(v.tensor_tensor(diff, w0, w1, ALU.subtract))
                ch.step(v.tensor_tensor(diff, diff, sel, ALU.mult))
                ch.mark(v.tensor_tensor(slot_w[par][:, :], diff, w1, ALU.add))
                ch.mark(v.tensor_tensor(y_at[par][:, :], num, none, ALU.add))
                dve.wait_ge(s["slot_step"], ch.base + SLOT_STEPS)
                ch.end()
                for i in range(3):
                    j0, j1 = 4 * i, min(4 * i + 4, J)
                    n = j1 - j0
                    dve.wait_ge(s["down_done"], J * e + j1)
                    v.tensor_tensor(y_s[par][:, j0:j1, :], bank[6 + i % 2][:, 0:n * D].rearrange("p (j d) -> p j d", j=n),
                                    pj_b[:, bass.ds(e, 1), :].to_broadcast([P, n, D]), ALU.add).then_inc(s["y_step"], 1)
                    dve.wait_ge(s["y_step"], 3 * e + i + 1)
                    v.tensor_tensor(y_s[par][:, j0:j1, :], y_s[par][:, j0:j1, :],
                                    slot_w[par][:, j0:j1].rearrange("p (j a) -> p j a", a=1).to_broadcast([P, n, D]), ALU.mult).then_inc(s["y_done"], 1)

            dve.wait_ge(s["ffn_loaded"], 32)
            experts(dve, expert)

        @block.tensor
        def _(pe):
            mm = nc.tensor.matmul

            def transposed(dst, src, done):
                for t in range(TG):
                    last = nc.tensor.transpose(dst[:, t * P:(t + 1) * P], src[:, t, 0:D], ident[:, :])
                last.then_inc(done, 1)

            def task_cT(g, par, ctx_count):
                pe.wait_ge(ctx_loaded[par], 16 * ctx_count)
                transposed(misc_a, ctx_s[par], s["cT_done"])

            def task_xT(g, par):
                pe.wait_ge(s["xn_done"], g + 1)
                transposed(misc_b, xn[par], s["xT_done"])

            def task_k(g):
                pe.wait_ge(s["cT_copied"], g + 1)
                mm(misc_a[:, :], wk_s, cT[:, :], start=True, stop=True).then_inc(s["k_done"], 1)

            def task_q(g):
                pe.wait_ge(s["xT_copied"], g + 1)
                pe.wait_ge(s["k_copied"], g + 1)
                mm(misc_a[:, :], wq_s, xT[:, :], start=True, stop=True).then_inc(s["q_done"], 1)

            def task_v(g):
                pe.wait_ge(s["q_copied"], 2 * (g + 1))
                w = wv_s.rearrange("p (j a c) -> p j a c", a=2, c=2 * DH)
                for b in range(BG):
                    for pp in range(2):
                        last = mm(misc_a[S * pp:S * (pp + 1), b * S:(b + 1) * S].rearrange("k (j c) -> k j c", j=TG),
                                  cT[:, b * S:(b + 1) * S], w[:, :, pp, :], start=True, stop=True)
                last.then_inc(s["v_done"], 1)

            def task_attn(g, par):
                pe.wait_ge(s["o_step"], 4 * (g + 1))
                for t in range(TG):
                    last = mm(misc_b[:, t * D:(t + 1) * D], oT[par][:, t * P:(t + 1) * P], wo_s, start=True, stop=True)
                last.then_inc(s["attn_done"], 1)

            def task_x2T(g, par):
                pe.wait_ge(s["row_done"], g + 1)
                transposed(misc_a, row[par], s["x2T_done"])

            def task_logits(g):
                pe.wait_ge(s["x2T_copied"], g + 1)
                pe.wait_ge(s["res_done"], g + 1)
                for t in range(TG):
                    for h in range(2):
                        last = mm(misc_b[S * h:S * (h + 1), t * E:(t + 1) * E], x2T[:, t * P + S * h:t * P + S * (h + 1)], gate_s[:, :],
                                  start=True, stop=True)
                last.then_inc(s["logits_done"], 1)

            def task_ranks(g):
                pe.wait_ge(s["route_step"], ROUTE_STEPS * (g + 1))
                c = 2 * E
                sg = signed[:, :, :, :].rearrange("p t k e -> p (t k e)")
                mm(misc_b[:, 0:TG * c], before[:, :], sg, start=True, stop=False, skip_group_check=True)
                for d in range(1, TG):
                    mm(misc_b[:, d * c:TG * c], all_ones[:, :], sg[:, 0:(TG - d) * c], start=False, stop=False, skip_group_check=True)
                for t in range(TG):
                    last = mm(misc_b[:, TG * c:(TG + 1) * c], all_ones[:, :], sg[:, t * c:(t + 1) * c],
                              start=False, stop=t == TG - 1, skip_group_check=True)
                last.then_inc(s["ranks_done"], 1)

            def scores(n, b, par):
                wait_later(pe, s["shifted"], n - 1)
                m = mask_rows[:, bass.ds(n, 1), :].to_broadcast([P, PAIRS, S])
                bank_ = score_bank[b % 2][:, :].rearrange("p (a k) -> p a k", k=S)
                mm(bank_, three_ones[:, :], m, start=True, stop=False)
                mm(bank_, q_blk[par][:, b, :, :].rearrange("p h q -> p (h q)"), k_blk[par][:, :, b * S:(b + 1) * S],
                   start=False, stop=True).then_inc(s["scores_done"], 1)

            def group_placed(half, par):
                pe.wait_ge(s["q_copied"], 2 * (2 * half + par + 1))
                pe.wait_ge(k_placed[par], 16 * PAIRS * (half + 1))

            def transpose_probs(n, b, first):
                pe.wait_ge(s["exp_done"], n + 1)
                if not (first and b == 0):
                    pe.wait_ge(s["probsT_copied"], n)
                for j in range(4):
                    last = nc.tensor.transpose(pt_bank[:, j * P:(j + 1) * P],
                                               probs[b % 4][:, 2 * j:2 * j + 2, :].rearrange("p a k -> p (a k)"), ident[:, :])
                last.then_inc(s["probsT_done"], 1)

            def heads(n, b, par, quad):
                pe.wait_ge(s["probsT_copied"], n + 1)
                q, into = b % 4, o_bank[b // 4]
                if q == 0:
                    wait_later(pe, s["o_step"], 2 * (quad - 1))
                    wait_later(pe, s["recipT_copied"], quad)
                for j in range(4):
                    mm(into[32 * j:32 * (j + 1), q * P:(q + 1) * P], v_blk[par][:, b, j, :, :].rearrange("k a c -> k (a c)"),
                       pT[b % 2][:, j * P:(j + 1) * P], start=True, stop=True)
                pe.wait_ge(s["recip_done"], n + 1)
                nc.tensor.transpose(r_bank[:, q * P:(q + 1) * P], recip_rows[b % 2][:, :, :, :].rearrange("p a h c -> p (a h c)"),
                                    ident[:, :]).then_inc(s["heads_done"], 1)

            pe.wait_ge(s["consts_made"], 5)
            task_xT(0, 0)
            task_cT(0, 0, 1)
            pe.wait_ge(s["w_loaded"], 16 * 4)
            task_k(0)
            task_q(0)
            task_v(0)
            pe.wait_ge(s["small_loaded"], 16 * 6)
            mm(misc_b[:, 0:D], cols[:, 2:3].to_broadcast([P, P]), wo_s, start=True, stop=True).then_inc(s["attn_done"], 1)
            pe.wait_ge(s["v_copied"], 2)
            pe.wait_ge(s["ones_made"], 2)
            pe.wait_ge(s["mask_placed"], 48)
            group_placed(0, 0)
            for n in range(AHEAD + 1):
                scores(n, n, 0)

            def body(g, half, par, first, last):
                nh, np_ = (half, 1) if par == 0 else (half + 1, 0)
                for b in range(BG):
                    n = BG * g + b
                    if b < BG - AHEAD - 1:
                        scores(n + AHEAD + 1, b + AHEAD + 1, par)
                    elif not last:
                        if b == BG - AHEAD - 1:
                            group_placed(nh, np_)
                        scores(n + AHEAD + 1, b + AHEAD + 1 - BG, np_)
                    transpose_probs(n, b, first)
                    if b == 0:
                        if not first:
                            heads(n - 1, BG - 1, 1 - par, None)
                    else:
                        heads(n - 1, b - 1, par, 2 * g + (b - 1) // 4)
                    at = LAST if last else MIDDLE
                    late = not (isinstance(g, int) and g < 2)
                    if b == at["logits"] and late:
                        wait_later(pe, s["place_step"], PLACE_STEPS * (g - 2))
                        task_logits(g - 2)
                    if not last:
                        if b == at["cT"]:
                            wait_later(pe, s["x2T_copied"], g - 1)
                            task_cT(g + 1, 1 - par, nh + 1)
                        if b == at["xT"]:
                            if first:
                                pe.wait_ge(s["out_bias_done"], 2)
                            wait_later(pe, s["route_step"], ROUTE_STEPS * (g - 1))
                            task_xT(g + 1, 1 - par)
                        if b == at["k"]:
                            task_k(g + 1)
                        if b == at["q"]:
                            task_q(g + 1)
                        if b == at["v"]:
                            task_v(g + 1)
                    if last and b == at["ranks"]:
                        task_ranks(g - 2)
                    if b == at["attn"] and not first:
                        if last:
                            pe.wait_ge(s["place_step"], PLACE_STEPS * (g - 1))
                        else:
                            pe.wait_ge(s["xT_copied"], g + 2)
                        task_attn(g - 1, 1 - par)
                    if not last and b == at["ranks"] and late:
                        pe.wait_ge(s["res_done"], g)
                        task_ranks(g - 2)
                    if b == at["x2T"] and not first:
                        pe.wait_ge(s["v_copied"], 2 * (g + 1) if last else 2 * (g + 2))
                        task_x2T(g - 1, 1 - par)
                    if last and b == at["logits1"]:
                        task_logits(g - 1)
                    if last and b == at["ranks1"]:
                        task_ranks(g - 1)

            groups(pe, body)
            heads(BG * GROUPS - 1, BG - 1, 1, None)
            g = GROUPS - 1
            pe.wait_ge(s["place_step"], PLACE_STEPS * g)
            task_attn(g, 1)
            task_x2T(g, 1)
            pe.wait_ge(s["res_done"], g + 1)
            task_logits(g)
            task_ranks(g)

            def slots_T(e, par, half, i):
                for j in range(4 * i, min(4 * i + 4, J)):
                    last = nc.tensor.transpose(bank[4 + i % 2][:, (j - 4 * i) * P:(j - 4 * i + 1) * P], xs[par][:, j, 0:D], ident[:, :])
                last.then_inc(s["xsT_done"], 1)

            def expert(e, half, par):
                pe.wait_ge(xs_loaded[par], 16 * (half + 1))
                for i in range(3):
                    if i < 2:
                        wait_later(pe, s["xsT_copied"], 3 * e)
                    else:
                        pe.wait_ge(s["xsT_copied"], 3 * e + 1)
                    slots_T(e, par, half, i)
                pe.wait_ge(fc_loaded[par], 16 * (half + 1))
                for c in range(HC):
                    for i, (a, b) in enumerate(((0, 512), (512, 1024), (1024, CAP))):
                        if c == 0:
                            pe.wait_ge(s["xsT_copied"], 3 * e + i + 1)
                        u = 3 * c + i
                        if u >= 4:
                            pe.wait_ge(s["gelu_done"], 3 * HC * e + u - 3)
                        mm(bank[u % 4][:, 0:b - a], fc_s[par][:, c * P:(c + 1) * P], xsT[:, a:b], start=True, stop=True).then_inc(s["up_done"], 1)
                pe.wait_ge(pj_loaded[par], 16 * (half + 1))
                for j in range(J):
                    if j % 4 == 0 and j:
                        pe.wait_ge(s["gelu_done"], 3 * HC * (e + 1) - 2 + min(j // 4, 2))
                    elif j == 0:
                        pe.wait_ge(s["gelu_done"], 3 * HC * (e + 1) - 2)
                    if j == 8:
                        pe.wait_ge(s["y_step"], 3 * e + 1)
                    for c in range(HC):
                        last = mm(bank[6 + (j // 4) % 2][:, (j % 4) * D:(j % 4 + 1) * D], hT[:, c, j * P:(j + 1) * P], pj_s[par][:, c, :],
                                  start=c == 0, stop=c == HC - 1)
                    last.then_inc(s["down_done"], 1)

            experts(pe, expert)


_INS = ["x", "ctx_1024", "mask_BxS2_ff1", "L0_xattn_Wq", "L0_xattn_bq", "L0_xattn_Wk", "L0_xattn_bk", "L0_xattn_Wv",
        "L0_xattn_bv", "L0_xattn_Wo", "L0_xattn_bo", "L0_ffn_gate_w", "L0_ffn_c_fc", "L0_ffn_fc_bias",
        "L0_ffn_c_proj", "L0_ffn_proj_bias"]


def kernel(**inputs):
    import concourse.bacc as bacc
    from concourse.bass_utils import run_bass_kernel_spmd

    nc = bacc.Bacc("TRN2", target_bir_lowering=False, num_devices=1)
    arrays, args = {}, []
    for name in _INS:
        a = np.ascontiguousarray(inputs[name])
        if name == "L0_ffn_fc_bias":
            e, _, h = a.shape
            a = np.ascontiguousarray(a.reshape(e * (h // P), P).T)
        arrays[f"in_{name}"] = a
        args.append(nc.dram_tensor(f"in_{name}", a.shape, mybir.dt.from_np(a.dtype), kind="ExternalInput").ap())
    shape = inputs["x"].shape
    args.append(nc.dram_tensor("out_x", shape, F32, kind="ExternalOutput").ap())
    xattn_moe(nc, *args)
    r = run_bass_kernel_spmd(nc, [arrays], core_ids=[0])
    return r.results[0]["out_x"]
```

```python
from contextlib import ExitStack

import concourse.bass as bass
import numpy as np
from concourse import mybir

F32 = mybir.dt.float32
F32R = mybir.dt.float32r
BF16 = mybir.dt.bfloat16
I32 = mybir.dt.int32
U32 = mybir.dt.uint32
ALU = mybir.AluOpType
ACT = mybir.ActivationFunctionType
AX = mybir.AxisListType

P = 128
TG = 4
NOWHERE = 1.0e6
EPS = 1e-5


def wait_before(engine, sem, value, met):
    if not isinstance(value, int):
        value = engine.compute_val(value)
    engine.wait_ge(met, 1)
    engine.wait_ge(sem, value)


def wait_later(engine, sem, value):
    if not isinstance(value, int) or value > 0:
        engine.wait_ge(sem, value)


class Chain:

    def __init__(self, engine, sem, per, turn):
        self.engine, self.sem, self.per, self.base, self.k = engine, sem, per, turn * per, 0

    def step(self, instruction):
        self.k += 1
        instruction.then_inc(self.sem, 1)
        self.engine.wait_ge(self.sem, self.base + self.k)

    def mark(self, instruction):
        self.k += 1
        instruction.then_inc(self.sem, 1)

    def end(self):
        assert self.k == self.per, (self.k, self.per)


def xattn_moe(nc, x, ctx_in, mask, wq, bq, wk, bk, wv, bv, wo, bo, gate_w, c_fc, fc_bias, c_proj, proj_bias, out):
    B, S, D = x.shape
    E, _, HID = c_fc.shape
    N = B * S
    H, DH = 16, D // 16
    PAIRS = H // 2
    GROUPS = N // (TG * P)
    TILES = N // P
    BG = TG * P // S
    TOK = TG * P
    CAP = int(1.25 * N * 2 / E)
    J = CAP // P
    SURE = 8
    HC = HID // P
    LINE = 2 * N
    ROW = D + 3
    SCALE = float(np.float32(1.0) / np.sqrt(np.float32(DH)))
    LOOPS = (GROUPS - 2) // 2
    assert S == 64 and D == P and CAP == J * P and GROUPS % 2 == 0 and E == 8

    x_v = x.rearrange("b s d -> (b s) d").rearrange("(t p) d -> p t d", p=P)
    ctx_v = ctx_in.rearrange("b s d -> (b s) d").rearrange("(t p) d -> p t d", p=P)
    out_v = out.rearrange("b s d -> (b s) d").rearrange("(t p) d -> p t d", p=P)
    lines = nc.dram_tensor("lines", [E * LINE, ROW], F32, kind="Internal").ap()
    lines_fill = lines.rearrange("(e l) r -> e l r", e=E)[:, N:N + CAP, :].rearrange("e (p j) r -> p e (j r)", p=P)
    out_rows = out.rearrange("b s d -> (b s) d")

    with ExitStack() as stack:
        def sb(name, shape, dt=F32):
            return stack.enter_context(nc.sbuf_tensor(name, shape, dt))

        def sem(name):
            return stack.enter_context(nc.semaphore(name))

        bank = [stack.enter_context(nc.psum_tensor(f"bank{i}", [P, 512], F32)) for i in range(8)]
        score_bank, pt_bank, r_bank, o_bank, misc_a, misc_b = bank[0:2], bank[2], bank[3], bank[4:6], bank[6], bank[7]

        ident = sb("ident", [P, P])
        mask_rows = sb("mask_rows", [P, B, S], BF16)
        three_ones = sb("three_ones", [P, P], BF16)
        before = sb("before", [P, P], BF16)
        all_ones = sb("all_ones", [P, P], BF16)
        iota8 = sb("iota8", [P, E])
        sign = sb("sign", [P, 2, E])
        number = sb("number", [P, TILES])
        slot = sb("slot", [P, J])
        middle = sb("middle", [P, E])
        next_row = sb("next_row", [P, 2, E])
        eps_t = sb("eps_t", [P, TILES])
        half_t = sb("half_t", [P, TILES])
        gelu_of = sb("gelu_of", [P, 1])
        minus_t = sb("minus_t", [P, TG])
        w_in = sb("w_in", [P, 4, D])
        wq_s, wk_s, wv_s, wo_s = (w_in[:, i, :] for i in range(4))
        gate_s = sb("gate_s", [P, E])
        cols = sb("cols", [P, 3])
        q_scale = sb("q_scale", [P, 2])
        q_bias = sb("q_bias", [P, 2])
        bo_b = sb("bo_b", [P, D])
        out_bias = sb("out_bias", [P, D])
        mask_in = sb("mask_in", [B, S])
        mask_f = sb("mask_f", [B, 2, S])
        mask_p = sb("mask_p", [B, 3, S], BF16)
        fc_b = sb("fc_b", [P, E * HC])
        fc_e = [sb(f"fc_e{i}", [P, HC]) for i in range(2)]
        pj_b = sb("pj_b", [P, E, D])

        res = sb("res", [P, TILES, D])
        stats = sb("stats", [P, TILES, 6])
        ln = sb("ln", [P, 4, TILES])
        mean1, rstd1 = ln[:, 0, :], ln[:, 3, :]
        ctx_s = [sb(f"ctx_s{i}", [P, TG, D]) for i in range(2)]
        xn = [sb(f"xn{i}", [P, TG, D]) for i in range(2)]
        xT = sb("xT", [P, TOK])
        cT = sb("cT", [P, TOK])
        kT = sb("kT", [P, TOK])
        q_blk = [sb(f"q_blk{i}", [P, BG, 2, S]) for i in range(2)]
        k_blk = [sb(f"k_blk{i}", [P, PAIRS, TOK]) for i in range(2)]
        v_blk = [sb(f"v_blk{i}", [P, BG, TG, 2, 2 * DH]) for i in range(2)]
        top = sb("top", [P, 4, PAIRS])
        probs = [sb(f"probs{i}", [P, PAIRS, S]) for i in range(4)]
        total = sb("total", [P, 4, PAIRS])
        recip = sb("recip", [P, 4, PAIRS])
        half_rows = sb("half_rows", [P, 2, DH])
        recip_rows = [sb(f"recip_rows{i}", [P, PAIRS, 2, DH]) for i in range(2)]
        pT = [sb(f"pT{i}", [P, 512]) for i in range(2)]
        rT = sb("rT", [P, 512])
        o_mul = [sb(f"o_mul{i}", [P, 4, 2, S]) for i in range(2)]
        oT = [sb(f"oT{i}", [P, TOK]) for i in range(2)]

        row = [sb(f"row{i}", [P, TG, ROW]) for i in range(2)]
        rows_at = [sb(f"rows_at{i}", [P, TG, 2], I32) for i in range(2)]
        stats2 = sb("stats2", [P, TG, 6])
        aggr2 = sb("aggr2", [P, TG, 2])
        rstd2 = sb("rstd2", [P, 4, TG])
        x2T = sb("x2T", [P, TOK])
        logits = sb("logits", [P, TG, E])
        best = sb("best", [P, TG, 8])
        best_at = sb("best_at", [P, TG, 8], U32)
        chosen = sb("chosen", [P, TG, 2, E], BF16)
        signed = sb("signed", [P, TG, 2, E], BF16)
        gap = sb("gap", [P, 3, TG])
        place = sb("place", [P, TG, 2, E])
        place_f = sb("place_f", [P, TG, 2])

        start_i = sb("start_i", [P, E], I32)
        long_bit = sb("long_bit", [P, E])
        is_long = sb("is_long", [P, E])
        long_f = sb("long_f", [P, 1])
        long_i = sb("long_i", [P, 1], I32)
        n_first = sb("n_first", [P, E])
        n_all = sb("n_all", [P, E])
        first_f = sb("first_f", [P, E])
        xs = [sb(f"xs{i}", [P, J, ROW]) for i in range(2)]
        fc_s = [sb(f"fc_s{i}", [P, HID]) for i in range(2)]
        pj_s = [sb(f"pj_s{i}", [P, HC, D]) for i in range(2)]
        xsT = [[sb(f"xsT{i}_{part}", [P, CAP], F32R) for part in ("high", "low")] for i in range(2)]
        fc_r = [[sb(f"fc_r{i}_{part}", [P, HID], F32R) for part in ("high", "low")] for i in range(2)]
        hT = sb("hT", [P, HC, CAP])
        y_s = [k_blk[0][:, 0:3, :].rearrange("p a b -> p (a b)")[:, 0:CAP].rearrange("p (j d) -> p j d", d=D),
               k_blk[0][:, 4:7, :].rearrange("p a b -> p (a b)")[:, 0:CAP].rearrange("p (j d) -> p j d", d=D)]
        y_at = [sb(f"y_at{i}", [P, J], I32) for i in range(2)]
        slot_w = [sb(f"slot_w{i}", [P, J]) for i in range(2)]
        slot_t = sb("slot_t", [P, 4, J])
        fill = xs[0]

        names = """bo_loaded gate_loaded w_loaded wk_loaded small_loaded x_loaded0 x_loaded ctx_loaded0 ctx_loaded1 k_placed0 k_placed1 mask_placed stats_done ones_made
            consts_made fill_made filled setup out_bias_done heads_made inverted ln1_step rstd1_half rstd1_done rstd2_half centred
            xn_done xT_done cT_done k_done q_done v_done attn_done x2T_done logits_done ranks_done bias_done ffn_loaded keys_cleared0 keys_cleared1 values_cleared
            xT_copied cT_copied k_copied q_copied v_copied x2T_copied biased
            scores_done top_done shifted exp_done sum_step recip_done probsT_done probsT_copied
            heads_done recipT_copied tile_normalised x2T_half x2T_half_copied half_residual o_scaled o_joined res_done ln2_step rstd2_done row_done
            route_step chosen_done gap_exp place_step lines_written0 lines_written1
            window_step long_step long_done start_done xs_loaded0 xs_loaded1 fc_loaded0 fc_loaded1 pj_loaded0 pj_loaded1
            xsT_done xsT_step xsT_split fc_step fc_split up_done gelu_done down_done slot_step y_done y_step y_scattered0 y_scattered1
            stored""".split()
        s = {n: sem(n) for n in names}
        x_loaded0, ln1_step = s["x_loaded0"], s["ln1_step"]
        ctx_loaded, k_placed = [s["ctx_loaded0"], s["ctx_loaded1"]], [s["k_placed0"], s["k_placed1"]]
        lines_written, xs_loaded = [s["lines_written0"], s["lines_written1"]], [s["xs_loaded0"], s["xs_loaded1"]]
        fc_loaded, pj_loaded = [s["fc_loaded0"], s["fc_loaded1"]], [s["pj_loaded0"], s["pj_loaded1"]]
        piece_loaded = [sem(f"piece_loaded{i}") for i in range(2)]
        y_scattered = [s["y_scattered0"], s["y_scattered1"]]

        FILLED = 16

        def rows_scattered(half):
            return FILLED + 16 * 2 * TG * half

        AHEAD = 2
        LN1_STEPS, LN2_STEPS, ROUTE_STEPS, PLACE_STEPS, WINDOW_STEPS, SLOT_STEPS = 7, 8, 11, 7, 6, 6

        MIDDLE = dict(logits=0, choose=1, exp_gap=2, cT=0, xT=1, k=1, q=2, join1=2, attn=3, v=4, ranks=2, place=3, residual=5,
                      join0=6, normalise2=6, x2T=7)
        LAST = dict(logits=0, choose=1, exp_gap=2, ranks=1, place=2, join1=1, attn=2, residual=4, normalise2=6, x2T=7,
                    join0=6)

        def groups(engine, body):
            body(0, 0, 0, True, False)
            body(1, 0, 1, False, False)
            with engine.Fori(1, GROUPS // 2 - 1) as i:
                body(2 * i, i, 0, False, False)
                body(2 * i + 1, i, 1, False, False)
            body(GROUPS - 2, GROUPS // 2 - 1, 0, False, False)
            body(GROUPS - 1, GROUPS // 2 - 1, 1, False, True)

        PARTS = ((range(0, 4), 6), (range(4, SURE), 7), (range(SURE, J), 6))
        LAST_PARTS = ((range(0, 1), 6), (range(1, 2), 7), (range(2, 3), 4), (range(3, 4), 5),
                      (range(4, 6), 0), (range(6, SURE), 1), (range(SURE, J), 2))

        def experts(engine, body):
            body(0, 0, 0, False)
            body(1, 0, 1, False)
            with engine.Fori(1, E // 2 - 1) as i:
                body(2 * i, i, 0, False)
                body(2 * i + 1, i, 1, False)
            body(E - 2, E // 2 - 1, 0, False)
            body(E - 1, E // 2 - 1, 1, True)

        block = stack.enter_context(nc.Block())

        @block.sync
        def _(sp):
            def load_ctx(g, par):
                sp.dma_start(ctx_s[par][:, :, :], ctx_v[:, bass.ds(g * TG, TG), :]).then_inc(ctx_loaded[par], 16)

            def store_residual(g):
                wait_before(sp, s["res_done"], g + 1, s["consts_made"])
                sp.dma_start(out_v[:, bass.ds(g * TG, TG), :], res[:, bass.ds(g * TG, TG), :]).then_inc(s["stored"], 16)

            def place_keys(g, par):
                wait_before(sp, s["k_copied"], g + 1, s["consts_made"])
                for pair in range(PAIRS):
                    r = slice(2 * DH * pair, 2 * DH * (pair + 1))
                    sp.dma_start(k_blk[par][r, pair, :], kT[r, :]).then_inc(k_placed[par], 16)

            load_ctx(0, 0)
            sp.dma_start(res[:, 0:TG, :], x_v[:, 0:TG, :]).then_inc(x_loaded0, 16)
            sp.dma_start(wk_s, wk).then_inc(s["wk_loaded"], 16)
            for i, w in ((0, wq), (2, wv), (3, wo)):
                sp.dma_start(w_in[:, i, :], w).then_inc(s["w_loaded"], 16)
            sp.dma_start(res[:, TG:TILES, :], x_v[:, TG:TILES, :]).then_inc(s["x_loaded"], 16)
            load_ctx(1, 1)
            sp.wait_ge(s["consts_made"], 1)
            sp.wait_ge(s["keys_cleared0"], 1)
            place_keys(0, 0)
            sp.dma_start(fc_b[:, :], fc_bias).then_inc(s["ffn_loaded"], 16)
            sp.dma_start(pj_b[:, :, :], proj_bias.rearrange("e a d -> a e d").to_broadcast([P, E, D])).then_inc(s["ffn_loaded"], 16)
            sp.wait_ge(s["fill_made"], 2)
            for e in range(2, E):
                sp.dma_start(lines_fill[:, e, :], fill[:, :, :].rearrange("p j r -> p (j r)")).then_inc(s["filled"], 16)

            def body(g, half, par, first, last):
                if not (last or first):
                    wait_before(sp, s["cT_done"], g, s["consts_made"])
                    load_ctx(g + 1, 1 - par)
                if not last:
                    if not first:
                        wait_before(sp, s["scores_done"], BG * g, s["consts_made"])
                    place_keys(g + 1, 1 - par)
                if not first:
                    store_residual(g - 1)

            groups(sp, body)
            store_residual(GROUPS - 1)

            def load_weights(e, par):
                sp.dma_start(fc_s[par][:, :], c_fc.rearrange("e d h -> d e h")[:, bass.ds(e, 1), :].rearrange("d e h -> d (e h)")
                             ).then_inc(fc_loaded[par], 16)
                sp.dma_start(pj_s[par][:, :, :], c_proj.rearrange("e (c p) d -> p e c d", p=P)[:, bass.ds(e, 1), :, :]
                             .rearrange("p e c d -> p (e c) d")).then_inc(pj_loaded[par], 16)

            def window_start(e):
                return sp.value_load(start_i[0:1, bass.ds(e, 1)], min_val=0, max_val=E * LINE - CAP)

            def load_window(par, start):
                sp.dma_start(xs[par][:, :, :], lines[bass.ds(start, CAP), :].rearrange("(j p) r -> p j r", p=P)
                             ).then_inc(xs_loaded[par], 16)

            load_weights(0, 0)
            load_weights(1, 1)
            sp.wait_ge(s["start_done"], 1)
            starts = [window_start(e) for e in range(2)]
            for par in range(2):
                sp.wait_ge(lines_written[par], rows_scattered(GROUPS // 2))
            for i, (j0, j1) in enumerate(((0, 4), (4, 8), (8, J))):
                sp.dma_start(xs[0][:, j0:j1, :], lines[bass.ds(starts[0], CAP), :].rearrange("(j p) r -> p j r", p=P)[:, j0:j1, :]
                             ).then_inc(s["xs_loaded0"] if i == 2 else piece_loaded[i], 16)
            load_window(1, starts[1])
            with sp.Fori(0, E // 2 - 1) as i:
                for par in range(2):
                    e = 2 * i + par
                    wait_before(sp, s["slot_step"], SLOT_STEPS * (e + 1), s["consts_made"])
                    wait_before(sp, s["xsT_done"], 3 * (e + 1), s["consts_made"])
                    load_window(par, window_start(e + 2))
                    wait_before(sp, s["down_done"], J * (e + 1), s["consts_made"])
                    load_weights(e + 2, par)

            sp.wait_ge(s["stored"], 16 * GROUPS)

        @block.gpsimd
        def _(pool):
            pool.memset(ident[:, :], 0.0).then_inc(s["consts_made"], 1)
            pool.memset(before[:, :], 1.0).then_inc(s["consts_made"], 1)
            pool.wait_ge(s["consts_made"], 2)
            pool.affine_select(out=ident[:, :], in_=ident[:, :], compare_op=ALU.not_equal, fill=1.0, base=0,
                               pattern=[[-1, P]], channel_multiplier=1).then_inc(s["consts_made"], 1)
            pool.affine_select(out=before[:, :], in_=before[:, :], compare_op=ALU.is_gt, fill=0.0, base=0,
                               pattern=[[1, P]], channel_multiplier=-1).then_inc(s["consts_made"], 1)
            pool.memset(eps_t[:, :], EPS)
            pool.memset(minus_t[:, :], -1.0)
            pool.memset(half_t[:, :], -0.5).then_inc(s["consts_made"], 1)
            pool.wait_ge(s["consts_made"], 5)

            def rstd(variance, half, out_, n, gate, done):
                pool.tensor_tensor(half, variance, eps_t[:, 0:n], ALU.add).then_inc(s["rstd1_half"], 1)
                pool.wait_ge(s["rstd1_half"], gate)
                pool.tensor_tensor(out_, half, half_t[:, 0:n], ALU.pow).then_inc(done, 1)

            def normalise1(g, par):
                wait_later(pool, s["xT_done"], g - 1)
                x_g = res[:, bass.ds(g * TG, TG), :]
                m, q = (a[:, bass.ds(g * TG, TG)].rearrange("p (t b) -> p t b", b=1).to_broadcast([P, TG, D]) for a in (mean1, rstd1))
                pool.tensor_tensor(xn[par][:, :, :], x_g, m, ALU.subtract).then_inc(s["centred"], 1)
                pool.wait_ge(s["centred"], g)
                pool.tensor_tensor(xn[par][:, :, :], xn[par][:, :, :], q, ALU.mult).then_inc(s["xn_done"], 1)

            def bias_residual(g):
                if isinstance(g, int) and g == 0:
                    pool.wait_ge(s["xn_done"], 1)
                else:
                    wait_before(pool, s["centred"], g, s["consts_made"])
                r = res[:, bass.ds(g * TG, TG), :]
                pool.tensor_tensor(r, r, out_bias[:, :].rearrange("p (a d) -> p a d", a=1).to_broadcast([P, TG, D]), ALU.add).then_inc(s["biased"], 1)

            pool.memset(k_blk[0][:, :, :], 0.0).then_inc(s["keys_cleared0"], 1)
            pool.wait_ge(ln1_step, LN1_STEPS)
            rstd(ln[:, 1, 0:TG], ln[:, 2, 0:TG], ln[:, 3, 0:TG], TG, 1, s["rstd1_done"])
            for i in range(2):
                pool.memset(v_blk[i][:, :, :, :, :], 0.0).then_inc(s["values_cleared"], 1)
            pool.iota(iota8[:, :], pattern=[[1, E]], base=0, channel_multiplier=0, allow_small_or_imprecise_dtypes=True)
            pool.iota(next_row[:, :, :], pattern=[[1, 2], [LINE, E]], base=N - 1, channel_multiplier=0, allow_small_or_imprecise_dtypes=True)
            pool.iota(middle[:, :], pattern=[[LINE, E]], base=N, channel_multiplier=0, allow_small_or_imprecise_dtypes=True)
            pool.iota(number[:, :], pattern=[[P, TILES]], base=0, channel_multiplier=1, allow_small_or_imprecise_dtypes=True)
            pool.iota(slot[:, :], pattern=[[P, J]], base=0, channel_multiplier=1, allow_small_or_imprecise_dtypes=True)
            for e in range(E):
                pool.memset(long_bit[:, e:e + 1], float(2 ** e))
            pool.memset(all_ones[:, :], 1.0)
            pool.memset(sign[:, 0, :], -1.0)
            pool.memset(sign[:, 1, :], 1.0).then_inc(s["consts_made"], 1)
            pool.wait_ge(s["setup"], 4)
            for i in range(3):
                pool.dma_start(mask_rows[i:i + 1, :, :], mask_p[:, i, :]).then_inc(s["mask_placed"], 16)
            pool.memset(k_blk[1][:, :, :], 0.0).then_inc(s["keys_cleared1"], 1)
            pool.memset(fill[:, :, :], 0.0).then_inc(s["fill_made"], 1)
            pool.wait_ge(s["fill_made"], 1)
            pool.memset(fill[:, :, D + 2:D + 3], NOWHERE).then_inc(s["fill_made"], 1)
            pool.wait_ge(ln1_step, 2 * LN1_STEPS)
            rstd(ln[:, 1, TG:TILES], ln[:, 2, TG:TILES], ln[:, 3, TG:TILES], TILES - TG, 2, s["rstd1_done"])
            pool.wait_ge(s["rstd1_done"], 2)
            normalise1(1, 1)

            def route(g, half, par, tiles=range(TG)):
                wait_before(pool, s["place_step"], PLACE_STEPS * (g + 1), s["consts_made"])
                for t in tiles:
                    for k in range(2):
                        pool.indirect_dma_start(
                            lines, bass.IndirectOffsetOnAxis(ap=rows_at[par][:, t, k:k + 1], axis=0), row[par][:, t, :], None,
                            bounds_check=E * LINE - 1, oob_is_err=False).then_inc(lines_written[par], 16)

            def power2(g):
                pool.wait_ge(s["ln2_step"], LN2_STEPS * (g + 1))
                wait_later(pool, s["row_done"], g)
                pool.tensor_tensor(rstd2[:, 2, :], aggr2[:, :, 0], minus_t[:, :], ALU.mult)
                rstd(aggr2[:, :, 1], rstd2[:, 0, :], rstd2[:, 1, :], TG, g + 3, s["rstd2_half"])
                pool.wait_ge(s["rstd2_half"], g + 1)
                pool.tensor_tensor(rstd2[:, 3, :], rstd2[:, 1, :], rstd2[:, 2, :], ALU.mult).then_inc(s["rstd2_done"], 1)

            def spread(n, k):
                wait_later(pool, s["heads_done"], n - 1)
                pool.wait_ge(s["inverted"], n + 1)
                pool.tensor_tensor(recip_rows[k % 2][:, :, :, :].rearrange("p a h c -> p a (h c)"),
                                   recip[:, k % 4, :].rearrange("p (a b) -> p a b", b=1).to_broadcast([P, PAIRS, 2 * DH]),
                                   half_rows[:, :, :].rearrange("p (b h) c -> p b (h c)", b=1).to_broadcast([P, PAIRS, 2 * DH]),
                                   ALU.mult).then_inc(s["recip_done"], 1)

            def body(g, half, par, first, last):
                at = LAST if last else MIDDLE
                for b in range(BG):
                    n = BG * g + b
                    spread(n, b)
                    if TG <= b < (BG - 2 if last else BG) and not (isinstance(g, int) and g < 2):
                        route(g - 2, half - 1, par, (b - TG,))
                    if not (isinstance(g, int) and g + 2 >= GROUPS):
                        if b == 0:
                            normalise1(g + 2, par)
                        if b == 1:
                            if first:
                                pool.wait_ge(s["out_bias_done"], 2)
                            bias_residual(g + 2)
                    if first and b == 2:
                        bias_residual(0)
                    if first and b == 3:
                        bias_residual(1)
                    if first and b in (4, 5):
                        pool.wait_ge(s["fill_made"], 2)
                        pool.dma_start(lines_fill[:, b - 4, :], fill[:, :, :].rearrange("p j r -> p (j r)")
                                       ).then_inc(lines_written[b - 4], 16)
                    if isinstance(g, int) and g == 1 and b == BG - 1:
                        pool.wait_ge(s["filled"], 16 * (E - 2))
                        for line_written in lines_written:
                            pool.wait_ge(line_written, FILLED)
                    if b == at["residual"] and not first:
                        power2(g - 1)

            groups(pool, body)
            route(GROUPS - 3, 0, 1, range(TG - 2, TG))
            power2(GROUPS - 1)
            route(GROUPS - 2, 0, 0)
            route(GROUPS - 1, 0, 1)

            def scatter(e, half, par, last):
                pool.wait_ge(s["slot_step"], SLOT_STEPS * (e + 1))
                wait_later(pool, y_scattered[1 - par], 16 * J * (half + par))
                begins = [tiles[0] for tiles, _ in (LAST_PARTS if last else PARTS)]
                for j in range(J):
                    if j in begins:
                        wait_before(pool, s["y_done"], 3 * e + begins.index(j) + 1, s["consts_made"])
                    pool.indirect_dma_start(
                        out_rows, bass.IndirectOffsetOnAxis(ap=y_at[par][:, j:j + 1], axis=0), y_s[par][:, j, :], None,
                        bounds_check=N - 1, oob_is_err=False, compute_op=ALU.add).then_inc(y_scattered[par], 16)

            pool.wait_ge(s["stored"], 16 * GROUPS)
            experts(pool, scatter)
            for par in range(2):
                pool.wait_ge(y_scattered[par], 16 * J * E // 2)

        @block.scalar
        def _(act):
            for i, b_ in enumerate((bq, bk, bv)):
                act.dma_start(cols[:, i:i + 1], b_.rearrange("(p a) -> p a", a=1)).then_inc(s["small_loaded"], 16)
            act.dma_start(mask_in[:, :], mask).then_inc(s["small_loaded"], 16)

            def copy(dst, src, done, **bias):
                act.activation(dst, src, ACT.Identity, **bias).then_inc(done, 1)

            def copy_cT(g):
                act.wait_ge(s["cT_done"], g + 1)
                wait_later(act, s["v_done"], g)
                copy(cT[:, :], misc_a[:, :], s["cT_copied"])

            def copy_xT(g):
                act.wait_ge(s["xT_done"], g + 1)
                wait_later(act, s["q_done"], g)
                copy(xT[:, :], misc_b[:, :], s["xT_copied"])

            def copy_k(g, half, par):
                act.wait_ge(s["k_done"], g + 1)
                wait_later(act, k_placed[1 - par], 16 * PAIRS * (half if par == 0 else half + 1))
                copy(kT[:, :], misc_a[:, :], s["k_copied"], bias=cols[:, 1:2])

            def copy_q(g, par):
                act.wait_ge(s["q_done"], g + 1)
                for h2 in range(2):
                    copy(q_blk[par][:, :, h2, :], misc_a[:, :].rearrange("p (b q) -> p b q", b=BG), s["q_copied"],
                         bias=q_bias[:, h2:h2 + 1], scale=q_scale[:, h2:h2 + 1])

            def copy_v(g, par):
                act.wait_ge(s["v_done"], g + 1)
                for pp in range(2):
                    r = slice(S * pp, S * (pp + 1))
                    copy(v_blk[par][r, :, :, pp, :].rearrange("k b j c -> k (b j) c"),
                         misc_a[r, :].rearrange("k (a c) -> k a c", c=2 * DH), s["v_copied"])

            def exp(n, k):
                act.wait_ge(s["shifted"], n + 1)
                act.activation(probs[k % 4][:, :, :], probs[k % 4][:, :, :], ACT.Exp).then_inc(s["exp_done"], 1)

            def copy_probsT(n, b, first):
                act.wait_ge(s["probsT_done"], n + 1)
                if not (first and b < 2):
                    act.wait_ge(s["heads_done"], n - 1)
                copy(pT[b % 2][:, :], pt_bank[:, :], s["probsT_copied"])

            def copy_recipT(quad, first):
                act.wait_ge(s["heads_done"], 4 * (quad + 1))
                if not first:
                    act.wait_ge(s["o_scaled"], quad)
                copy(rT[:, :], r_bank[:, :], s["recipT_copied"])

            def copy_x2T(g):
                act.wait_ge(s["x2T_done"], g + 1)
                wait_later(act, s["logits_done"], g)
                copy(x2T[:, :], misc_a[:, :], s["x2T_copied"])

            def normalise2(g, half, par):
                act.wait_ge(s["rstd2_done"], g + 1)
                act.wait_ge(lines_written[par], rows_scattered(half))
                for t in range(TG):
                    last = act.activation(row[par][:, t, 0:D], res[:, bass.ds(g * TG + t, 1), :].rearrange("p a d -> p (a d)"),
                                          ACT.Identity, bias=rstd2[:, 3, t:t + 1], scale=rstd2[:, 1, t:t + 1])
                last.then_inc(s["row_done"], 1)

            def exp_gap(g):
                act.wait_ge(s["chosen_done"], g + 1)
                act.activation(gap[:, 1, :], gap[:, 0, :], ACT.Exp).then_inc(s["gap_exp"], 1)

            copy_cT(0)
            act.wait_ge(s["small_loaded"], 16 * 4)
            copy_k(0, 0, 0)
            act.dma_start(bo_b[:, :], bo.rearrange("(a d) -> a d", a=1).to_broadcast([P, D])).then_inc(s["bo_loaded"], 16)
            act.dma_start(gate_s[:, :], gate_w).then_inc(s["gate_loaded"], 16)
            copy_xT(0)
            act.wait_ge(s["setup"], 3)
            copy_q(0, 0)
            act.wait_ge(s["values_cleared"], 2)
            copy_v(0, 0)
            for n in range(AHEAD):
                exp(n, n)

            def body(g, half, par, first, last):
                for b in range(BG):
                    n = BG * g + b
                    at = LAST if last else MIDDLE
                    if b == 1 and not first:
                        copy_recipT(2 * g - 1, False)
                    if b == 5:
                        copy_recipT(2 * g, first)
                    copy_probsT(n, b, first)
                    if b == at["exp_gap"] and not (isinstance(g, int) and g < 2):
                        exp_gap(g - 2)
                    if not (last and b >= BG - AHEAD):
                        exp(n + AHEAD, b + AHEAD)
                    if not last:
                        if b == at["cT"]:
                            copy_cT(g + 1)
                        if b == at["xT"]:
                            copy_xT(g + 1)
                        if b == at["k"]:
                            copy_k(g + 1, half if par == 0 else half + 1, 1 - par)
                        if b == at["q"]:
                            copy_q(g + 1, 1 - par)
                        if b == at["v"]:
                            copy_v(g + 1, 1 - par)
                    if not first:
                        if b == at["normalise2"]:
                            normalise2(g - 1, half if par == 1 else half - 1, 1 - par)
                        if b == at["x2T"]:
                            copy_x2T(g - 1)

            groups(act, body)
            copy_recipT(2 * GROUPS - 1, False)
            exp_gap(GROUPS - 2)
            for h, half_bank in enumerate((misc_a, o_bank[1])):
                act.wait_ge(s["x2T_half"], h + 1)
                if h == 0:
                    act.wait_ge(s["logits_done"], GROUPS - 1)
                copy(x2T[:, 2 * h * P:2 * (h + 1) * P], half_bank[:, 0:2 * P], s["x2T_half_copied"])
            exp_gap(GROUPS - 1)

            act.activation(gelu_of[:, :], half_t[:, 0:1], ACT.Gelu)

            def gelus(e, half, par, last):
                act.wait_ge(s["bias_done"], e + 1)
                for i in range(3):
                    a, b = 512 * i, min(512 * (i + 1), CAP)
                    for c in range(HC):
                        act.wait_ge(s["up_done"], 3 * HC * e + HC * i + c + 1)
                        act.activation(hT[:, c, a:b], bank[c][:, 0:b - a], ACT.Gelu,
                                       bias=fc_e[par][:, c:c + 1]).then_inc(s["gelu_done"], 1)

            experts(act, gelus)

        @block.vector
        def _(dve):
            v = nc.vector
            v.memset(mask_rows[:, :, :], 0.0).then_inc(s["setup"], 1)

            def ln1(t0, t1, turn):
                ch = Chain(dve, ln1_step, LN1_STEPS, turn)
                m, var, tmp = ln[:, 0, t0:t1], ln[:, 1, t0:t1], ln[:, 2, t0:t1]
                st = stats[:, t0:t1, :]
                ch.step(v.tensor_tensor(m, st[:, :, 1], st[:, :, 4], ALU.add))
                ch.step(v.tensor_scalar(m, m, 0.5, None, ALU.mult))
                ch.step(v.tensor_tensor(tmp, st[:, :, 1], m, ALU.subtract))
                ch.step(v.tensor_tensor(tmp, tmp, tmp, ALU.mult))
                ch.step(v.tensor_tensor(var, st[:, :, 2], st[:, :, 5], ALU.add))
                ch.step(v.tensor_scalar(var, var, 1.0 / D, None, ALU.mult))
                ch.step(v.tensor_tensor(var, var, tmp, ALU.add))
                ch.end()

            dve.wait_ge(x_loaded0, 16)
            for t in range(TG):
                v.bn_stats(stats[:, t, :], res[:, t, :]).then_inc(s["stats_done"], 1)
            dve.wait_ge(s["stats_done"], TG)
            ln1(0, TG, 0)
            dve.wait_ge(s["rstd1_done"], 1)
            for t in range(TG):
                last = v.tensor_scalar(xn[0][:, t, :], res[:, t, :], mean1[:, t:t + 1], rstd1[:, t:t + 1], ALU.subtract, ALU.mult)
            last.then_inc(s["xn_done"], 1)
            dve.wait_ge(s["consts_made"], 5)
            v.reduce_sum(q_scale[:, :], ident[:, :].rearrange("p (a h d) -> p h a d", h=2, d=DH), AX.XY).then_inc(s["out_bias_done"], 1)
            dve.wait_ge(s["out_bias_done"], 1)
            v.tensor_scalar(q_scale[:, :], q_scale[:, :], SCALE, None, ALU.mult).then_inc(s["setup"], 1)
            dve.wait_ge(s["setup"], 2)
            dve.wait_ge(s["small_loaded"], 16 * 4)
            v.tensor_scalar(q_bias[:, :], q_scale[:, :], cols[:, 0:1], None, ALU.mult).then_inc(s["setup"], 1)
            mch = Chain(dve, s["window_step"], 6, 0)
            mch.step(v.tensor_scalar(mask_f[:, 0, :], mask_in[:, :], -1.0, 1.0, ALU.mult, ALU.add))
            mch.step(v.tensor_scalar(mask_f[:, 0, :], mask_f[:, 0, :], -1.0e30, None, ALU.mult))
            mch.step(v.tensor_copy(mask_p[:, 0, :], mask_f[:, 0, :]))
            mch.step(v.tensor_tensor(mask_f[:, 1, :], mask_f[:, 0, :], mask_p[:, 0, :], ALU.subtract))
            mch.step(v.tensor_copy(mask_p[:, 1, :], mask_f[:, 1, :]))
            mch.step(v.tensor_tensor(mask_f[:, 0, :], mask_f[:, 1, :], mask_p[:, 1, :], ALU.subtract))
            v.tensor_copy(mask_p[:, 2, :], mask_f[:, 0, :]).then_inc(s["setup"], 1)
            v.memset(three_ones[:, :], 0.0).then_inc(s["ones_made"], 1)
            dve.wait_ge(s["ones_made"], 1)
            v.memset(three_ones[0:3, :], 1.0).then_inc(s["ones_made"], 1)
            v.memset(half_rows[:, :, :], 0.0).then_inc(s["heads_made"], 1)
            dve.wait_ge(s["heads_made"], 1)
            for h2 in range(2):
                v.memset(half_rows[S * h2:S * (h2 + 1), h2, :], 1.0).then_inc(s["heads_made"], 1)
            dve.wait_ge(s["heads_made"], 3)
            dve.wait_ge(s["x_loaded"], 16)
            for t in range(TG, TILES):
                v.bn_stats(stats[:, t, :], res[:, t, :]).then_inc(s["stats_done"], 1)
            dve.wait_ge(s["stats_done"], TILES)
            ln1(TG, TILES, 1)

            def top_of(n, k):
                dve.wait_ge(s["scores_done"], n + 1)
                sc = score_bank[k % 2][:, :].rearrange("p (a k) -> p a k", k=S)
                v.reduce_max(top[:, k % 4, :], sc, AX.X).then_inc(s["top_done"], 1)

            def shift(n, k):
                sc = score_bank[k % 2][:, :].rearrange("p (a k) -> p a k", k=S)
                wait_later(dve, s["probsT_done"], n - 3)
                dve.wait_ge(s["top_done"], n + 1)
                v.tensor_tensor(probs[k % 4][:, :, :], sc,
                                top[:, k % 4, :].rearrange("p (a b) -> p a b", b=1).to_broadcast([P, PAIRS, S]),
                                ALU.subtract).then_inc(s["shifted"], 1)

            def sums(n, k):
                dve.wait_ge(s["exp_done"], n + 1)
                v.reduce_sum(total[:, k % 4, :], probs[k % 4][:, :, :], AX.X).then_inc(s["sum_step"], 1)

            def invert(n, k):
                dve.wait_ge(s["sum_step"], n + 1)
                v.reciprocal(recip[:, k % 4, :], total[:, k % 4, :]).then_inc(s["inverted"], 1)

            def scale_heads(quad, q2):
                dve.wait_ge(s["recipT_copied"], quad + 1)
                v.tensor_tensor(o_mul[q2][:, :, :, :].rearrange("p b h q -> p (b h q)"), o_bank[q2][:, :], rT[:, :], ALU.mult).then_inc(s["o_scaled"], 1)

            def join_heads(quad, par, q2):
                dve.wait_ge(s["o_scaled"], quad + 1)
                v.tensor_tensor(oT[par][:, q2 * 256:(q2 + 1) * 256].rearrange("p (b q) -> p b q", b=4),
                                o_mul[q2][:, :, 0, :], o_mul[q2][:, :, 1, :], ALU.add).then_inc(s["o_joined"], 1)

            def residual(g):
                dve.wait_ge(s["attn_done"], g + 2)
                dve.wait_ge(s["biased"], g + 1)
                r = res[:, bass.ds(g * TG, TG), :]
                v.tensor_tensor(r, misc_b[:, :].rearrange("p (t d) -> p t d", t=TG), r, ALU.add).then_inc(s["res_done"], 1)

            def statistics(g):
                wait_before(dve, s["res_done"], g + 1, s["setup"])
                for t in range(TG):
                    v.bn_stats(stats2[:, t, :], res[:, bass.ds(g * TG + t, 1), :].rearrange("p a d -> p (a d)")).then_inc(s["ln2_step"], 1)

            def residual_half(g, h, from_bank):
                dve.wait_ge(s["attn_done"], g + 2 + h)
                dve.wait_ge(s["biased"], g + 1)
                t0 = g * TG + 2 * h
                r = res[:, t0:t0 + 2, :]
                v.tensor_tensor(r, from_bank[:, 0:2 * D].rearrange("p (t d) -> p t d", t=2), r, ALU.add
                                ).then_inc(s["res_done"] if h else s["half_residual"], 1)
                if h:
                    dve.wait_ge(s["res_done"], g + 1)
                else:
                    dve.wait_ge(s["half_residual"], 1)
                for t in range(2):
                    v.bn_stats(stats2[:, 2 * h + t, :], res[:, t0 + t, :]).then_inc(s["ln2_step"], 1)

            def mean_variance(g):
                wait_before(dve, s["ln2_step"], LN2_STEPS * g + TG, s["setup"])
                for t in range(TG):
                    v.bn_aggr(aggr2[:, t, :], stats2[:, t, :]).then_inc(s["ln2_step"], 1)

            def read_logits(g):
                dve.wait_ge(s["logits_done"], g + 1)
                v.tensor_copy(logits[:, :, :].rearrange("p t e -> p (t e)"), misc_b[:, 0:TG * E]).then_inc(s["route_step"], 1)

            def best_logits(g):
                wait_before(dve, s["route_step"], ROUTE_STEPS * g + 1, s["setup"])
                for t in range(TG):
                    v.max(best[:, t, :], logits[:, t, :]).then_inc(s["route_step"], 1)

            def best_experts(g):
                wait_before(dve, s["route_step"], ROUTE_STEPS * g + 1 + TG, s["setup"])
                for t in range(TG):
                    v.max_index(best_at[:, t, :], best[:, t, :], logits[:, t, :]).then_inc(s["route_step"], 1)

            def choose(g):
                dve.wait_ge(s["route_step"], ROUTE_STEPS * g + 1 + 2 * TG)
                v.tensor_tensor(chosen[:, :, :, :],
                                best_at[:, :, 0:2].rearrange("p t (k a) -> p t k a", a=1).to_broadcast([P, TG, 2, E]),
                                iota8[:, :].rearrange("p (a b e) -> p a b e", a=1, b=1).to_broadcast([P, TG, 2, E]),
                                ALU.is_equal).then_inc(s["route_step"], 1)
                v.tensor_tensor(gap[:, 0, :], best[:, :, 1], best[:, :, 0], ALU.subtract).then_inc(s["chosen_done"], 1)

            def sign_choice(g):
                dve.wait_ge(s["route_step"], ROUTE_STEPS * g + 2 + 2 * TG)
                v.tensor_tensor(signed[:, :, :, :].rearrange("p t k e -> p t (k e)"), chosen[:, :, :, :].rearrange("p t k e -> p t (k e)"),
                                sign[:, :, :].rearrange("p k e -> p (k e)").rearrange("p (a c) -> p a c", a=1).to_broadcast([P, TG, 2 * E]),
                                ALU.mult).then_inc(s["route_step"], 1)

            nr = next_row[:, :, :].rearrange("p k e -> p (k e)")

            def rows_by_expert(g, ranks=misc_b):
                dve.wait_ge(s["ranks_done"], g + 1)
                v.tensor_tensor(place[:, :, :, :].rearrange("p t k e -> p t (k e)"),
                                ranks[:, 0:TG * 2 * E].rearrange("p (t c) -> p t c", t=TG),
                                nr.rearrange("p (a c) -> p a c", a=1).to_broadcast([P, TG, 2 * E]), ALU.add).then_inc(s["place_step"], 1)
                dve.wait_ge(s["place_step"], PLACE_STEPS * g + 1)
                v.tensor_tensor(nr, ranks[:, TG * 2 * E:(TG + 1) * 2 * E], nr, ALU.add).then_inc(s["place_step"], 1)

            def rows_of_choice(g):
                v.tensor_tensor(place[:, :, :, :], place[:, :, :, :], chosen[:, :, :, :], ALU.mult).then_inc(s["place_step"], 1)

            def sum_rows(g):
                dve.wait_ge(s["place_step"], PLACE_STEPS * g + 3)
                v.reduce_sum(place_f[:, :, :], place[:, :, :, :], AX.X).then_inc(s["place_step"], 1)
                dve.wait_ge(s["gap_exp"], g + 1)
                v.tensor_scalar(gap[:, 2, :], gap[:, 1, :], 1.0, None, ALU.add).then_inc(s["place_step"], 1)

            def first_weight(g, par):
                dve.wait_ge(s["place_step"], PLACE_STEPS * g + 5)
                v.tensor_copy(rows_at[par][:, :, :], place_f[:, :, :])
                v.reciprocal(row[par][:, :, D], gap[:, 2, :]).then_inc(s["place_step"], 1)

            def second_weight(g, par):
                dve.wait_ge(s["place_step"], PLACE_STEPS * g + 6)
                v.tensor_copy(row[par][:, :, D + 2], number[:, bass.ds(g * TG, TG)])
                v.tensor_tensor(row[par][:, :, D + 1], row[par][:, :, D], gap[:, 1, :], ALU.mult).then_inc(s["place_step"], 1)

            def residual_at_once(g):
                residual(g)
                statistics(g)
                mean_variance(g)

            def choose_at_once(g):
                read_logits(g)
                best_logits(g)
                best_experts(g)
                choose(g)
                sign_choice(g)

            def place_at_once(g, par, ranks=misc_b):
                rows_by_expert(g, ranks)
                rows_of_choice(g)
                sum_rows(g)
                first_weight(g, par)
                second_weight(g, par)

            for n in range(AHEAD):
                top_of(n, n)
                shift(n, n)
            dve.wait_ge(s["attn_done"], 1)
            dve.wait_ge(s["bo_loaded"], 16)
            v.tensor_tensor(out_bias[:, :], misc_b[:, 0:D], bo_b[:, :], ALU.add).then_inc(s["out_bias_done"], 1)

            def body(g, half, par, first, last):
                for b in range(BG):
                    n = BG * g + b
                    at = LAST if last else MIDDLE
                    more = not (last and b >= BG - AHEAD)
                    late = not (isinstance(g, int) and g < 2)
                    chain = {} if last else dict(choose=at["choose"] + 1, place=at["place"] + 1, residual=at["residual"])
                    choosing = late and b == chain.get("choose")
                    placing = late and b == chain.get("place")
                    adding = not first and b == chain.get("residual")
                    if more:
                        top_of(n + AHEAD, b + AHEAD)
                    if b == at["join1"] + 1 and not first:
                        join_heads(2 * g - 1, 1 - par, 1)
                    if b == at["join0"] + 1:
                        join_heads(2 * g, par, 0)
                    if adding:
                        residual(g - 1)
                    if choosing:
                        best_logits(g - 2)
                    if placing:
                        rows_of_choice(g - 2)
                    sums(n, b)
                    if adding:
                        statistics(g - 1)
                    if choosing:
                        best_experts(g - 2)
                    if placing:
                        sum_rows(g - 2)
                    if more:
                        shift(n + AHEAD, b + AHEAD)
                    if adding:
                        mean_variance(g - 1)
                    if choosing:
                        choose(g - 2)
                    if placing:
                        first_weight(g - 2, par)
                    invert(n, b)
                    if choosing:
                        sign_choice(g - 2)
                    if placing:
                        second_weight(g - 2, par)
                    if b == at["choose"] and late:
                        if last:
                            choose_at_once(g - 2)
                        else:
                            read_logits(g - 2)
                    if b == at["place"] and late:
                        if last:
                            place_at_once(g - 2, par)
                        else:
                            rows_by_expert(g - 2)
                    if b == at["join1"] and not first:
                        scale_heads(2 * g - 1, 1)
                    if b == at["join0"]:
                        scale_heads(2 * g, 0)
                    if last and b == at["residual"]:
                        residual_at_once(g - 1)

            groups(dve, body)
            residual_half(GROUPS - 1, 0, score_bank[1])
            scale_heads(2 * GROUPS - 1, 1)
            join_heads(2 * GROUPS - 1, 1, 1)
            read_logits(GROUPS - 2)
            best_logits(GROUPS - 2)
            best_experts(GROUPS - 2)
            choose(GROUPS - 2)
            sign_choice(GROUPS - 2)
            residual_half(GROUPS - 1, 1, o_bank[0])
            mean_variance(GROUPS - 1)
            place_at_once(GROUPS - 2, 0, score_bank[0])
            g = GROUPS - 1
            dve.wait_ge(s["rstd2_done"], g + 1)
            dve.wait_ge(lines_written[1], rows_scattered(GROUPS // 2 - 1))
            for t in range(TG):
                v.tensor_scalar(row[1][:, t, 0:D], res[:, g * TG + t, :], rstd2[:, 1, t:t + 1], rstd2[:, 3, t:t + 1], ALU.mult, ALU.add
                                ).then_inc(s["tile_normalised"], 1)
            choose_at_once(GROUPS - 1)
            place_at_once(GROUPS - 1, 1)

            wch = Chain(dve, s["window_step"], WINDOW_STEPS, 1)
            wch.step(v.tensor_scalar(first_f[:, :], middle[:, :], -float(CAP), None, ALU.add))
            wch.step(v.tensor_scalar(n_all[:, :], next_row[:, 0, :], 1.0, None, ALU.add))
            wch.step(v.tensor_tensor(first_f[:, :], first_f[:, :], n_all[:, :], ALU.max))
            v.tensor_copy(start_i[:, :], first_f[:, :]).then_inc(s["start_done"], 1)
            wch.step(v.tensor_tensor(n_first[:, :], middle[:, :], first_f[:, :], ALU.subtract))
            wch.step(v.tensor_tensor(n_all[:, :], next_row[:, 1, :], middle[:, :], ALU.subtract))
            wch.step(v.tensor_tensor(n_all[:, :], n_all[:, :], n_first[:, :], ALU.add))
            wch.end()
            lch = Chain(dve, s["long_step"], 3, 0)
            lch.step(v.tensor_scalar(is_long[:, :], n_all[:, :], float(SURE * P), None, ALU.is_gt))
            lch.step(v.tensor_tensor(is_long[:, :], is_long[:, :], long_bit[:, :], ALU.mult))
            lch.step(v.reduce_sum(long_f[:, :], is_long[:, :], AX.X))
            lch.end()
            v.tensor_copy(long_i[:, :], long_f[:, :]).then_inc(s["long_done"], 1)

            def split_weights(e, half, par):
                high, low = (part[:, :] for part in fc_r[par])
                dve.wait_ge(fc_loaded[par], 16 * (half + 1))
                v.tensor_copy(high, fc_s[par][:, :]).then_inc(s["fc_step"], 1)
                v.tensor_copy(fc_e[par][:, :], fc_b[:, bass.ds(e * HC, HC)]).then_inc(s["bias_done"], 1)
                dve.wait_ge(s["fc_step"], e + 1)
                v.tensor_tensor(low, fc_s[par][:, :], high, ALU.subtract).then_inc(s["fc_split"], 1)

            def split_tokens(e, par, i):
                a, b = 512 * i, min(512 * (i + 1), CAP)
                high, low = (part[:, a:b] for part in xsT[par])
                dve.wait_ge(s["xsT_done"], 3 * e + i + 1)
                wait_later(dve, s["up_done"], 3 * HC * (e - 1))
                v.tensor_copy(high, bank[4 + i % 2][:, 0:b - a]).then_inc(s["xsT_step"], 1)
                dve.wait_ge(s["xsT_step"], 3 * e + i + 1)
                v.tensor_tensor(low, bank[4 + i % 2][:, 0:b - a], high, ALU.subtract).then_inc(s["xsT_split"], 1)

            def weigh(e, par, k, tiles, in_bank):
                j0, n = tiles[0], len(tiles)
                j1 = j0 + n
                dve.wait_ge(s["down_done"], J * e + j1)
                v.tensor_tensor(y_s[par][:, j0:j1, :], bank[in_bank][:, 0:n * D].rearrange("p (j d) -> p j d", j=n),
                                pj_b[:, bass.ds(e, 1), :].to_broadcast([P, n, D]), ALU.add).then_inc(s["y_step"], 1)
                dve.wait_ge(s["y_step"], 3 * e + k + 1)
                v.tensor_tensor(y_s[par][:, j0:j1, :], y_s[par][:, j0:j1, :],
                                slot_w[par][:, j0:j1].rearrange("p (j a) -> p j a", a=1).to_broadcast([P, n, D]), ALU.mult).then_inc(s["y_done"], 1)

            def weigh_slots(e, half, par):
                wait_later(dve, y_scattered[par], 16 * J * half)
                if isinstance(e, int) and e == 0:
                    for piece in piece_loaded:
                        dve.wait_ge(piece, 16)
                dve.wait_ge(xs_loaded[par], 16 * (half + 1))
                w0, w1, num = (xs[par][:, :, D + i] for i in range(3))
                sel, diff, none = (slot_t[:, i, :] for i in range(3))
                ch = Chain(dve, s["slot_step"], SLOT_STEPS, e)
                ch.mark(v.tensor_scalar(sel, slot[:, :], n_first[:, bass.ds(e, 1)], None, ALU.is_lt))
                ch.mark(v.tensor_scalar(none, slot[:, :], n_all[:, bass.ds(e, 1)], NOWHERE, ALU.is_ge, ALU.mult))
                ch.step(v.tensor_tensor(diff, w0, w1, ALU.subtract))
                ch.step(v.tensor_tensor(diff, diff, sel, ALU.mult))
                ch.mark(v.tensor_tensor(slot_w[par][:, :], diff, w1, ALU.add))
                ch.mark(v.tensor_tensor(y_at[par][:, :], num, none, ALU.add))
                dve.wait_ge(s["slot_step"], ch.base + SLOT_STEPS)
                ch.end()

            def expert(e, half, par, last):
                weigh_slots(e, half, par)
                if not last:
                    nh = half if par == 0 else half + 1
                    split_weights(e + 1, nh, 1 - par)
                    split_tokens(e + 1, 1 - par, 0)
                    split_tokens(e + 1, 1 - par, 1)
                for k, (tiles, in_bank) in enumerate(LAST_PARTS if last else PARTS):
                    weigh(e, par, k, tiles, in_bank)
                    if k == 0 and not last:
                        split_tokens(e + 1, 1 - par, 2)

            dve.wait_ge(s["ffn_loaded"], 32)
            split_weights(0, 0, 0)
            for i in range(3):
                split_tokens(0, 0, i)
            experts(dve, expert)

        @block.tensor
        def _(pe):
            mm = nc.tensor.matmul

            def transposed(dst, src, done):
                for t in range(TG):
                    last = nc.tensor.transpose(dst[:, t * P:(t + 1) * P], src[:, t, 0:D], ident[:, :])
                last.then_inc(done, 1)

            def task_cT(g, par, ctx_count):
                pe.wait_ge(ctx_loaded[par], 16 * ctx_count)
                transposed(misc_a, ctx_s[par], s["cT_done"])

            def task_xT(g, par):
                pe.wait_ge(s["xn_done"], g + 1)
                transposed(misc_b, xn[par], s["xT_done"])

            def task_k(g):
                pe.wait_ge(s["cT_copied"], g + 1)
                mm(misc_a[:, :], wk_s, cT[:, :], start=True, stop=True).then_inc(s["k_done"], 1)

            def task_q(g):
                pe.wait_ge(s["xT_copied"], g + 1)
                pe.wait_ge(s["k_copied"], g + 1)
                mm(misc_a[:, :], wq_s, xT[:, :], start=True, stop=True).then_inc(s["q_done"], 1)

            def task_v(g):
                pe.wait_ge(s["q_copied"], 2 * (g + 1))
                w = wv_s.rearrange("p (j a c) -> p j a c", a=2, c=2 * DH)
                for b in range(BG):
                    for pp in range(2):
                        last = mm(misc_a[S * pp:S * (pp + 1), b * S:(b + 1) * S].rearrange("k (j c) -> k j c", j=TG),
                                  cT[:, b * S:(b + 1) * S], w[:, :, pp, :], start=True, stop=True)
                last.then_inc(s["v_done"], 1)

            def task_attn(g, par):
                pe.wait_ge(s["o_joined"], 2 * (g + 1))
                for t in range(TG):
                    last = mm(misc_b[:, t * D:(t + 1) * D], oT[par][:, t * P:(t + 1) * P], wo_s, start=True, stop=True)
                last.then_inc(s["attn_done"], 1)

            def task_x2T(g, par):
                pe.wait_ge(s["row_done"], g + 1)
                transposed(misc_a, row[par], s["x2T_done"])

            def logits_of(tiles):
                for t in tiles:
                    for h in range(2):
                        last = mm(misc_b[S * h:S * (h + 1), t * E:(t + 1) * E], x2T[:, t * P + S * h:t * P + S * (h + 1)], gate_s[:, :],
                                  start=True, stop=True)
                return last

            def task_logits(g):
                pe.wait_ge(s["x2T_copied"], g + 1)
                pe.wait_ge(s["res_done"], g + 1)
                logits_of(range(TG)).then_inc(s["logits_done"], 1)

            def task_ranks(g, into=misc_b):
                pe.wait_ge(s["route_step"], ROUTE_STEPS * (g + 1))
                c = 2 * E
                sg = signed[:, :, :, :].rearrange("p t k e -> p (t k e)")
                mm(into[:, 0:TG * c], before[:, :], sg, start=True, stop=False, skip_group_check=True)
                for d in range(1, TG):
                    mm(into[:, d * c:TG * c], all_ones[:, :], sg[:, 0:(TG - d) * c], start=False, stop=False, skip_group_check=True)
                for t in range(TG):
                    last = mm(into[:, TG * c:(TG + 1) * c], all_ones[:, :], sg[:, t * c:(t + 1) * c],
                              start=False, stop=t == TG - 1, skip_group_check=True)
                last.then_inc(s["ranks_done"], 1)

            def scores(n, b, par):
                wait_later(pe, s["shifted"], n - 1)
                m = mask_rows[:, bass.ds(n, 1), :].to_broadcast([P, PAIRS, S])
                bank_ = score_bank[b % 2][:, :].rearrange("p (a k) -> p a k", k=S)
                mm(bank_, three_ones[:, :], m, start=True, stop=False)
                mm(bank_, q_blk[par][:, b, :, :].rearrange("p h q -> p (h q)"), k_blk[par][:, :, b * S:(b + 1) * S],
                   start=False, stop=True).then_inc(s["scores_done"], 1)

            def group_placed(half, par):
                pe.wait_ge(s["q_copied"], 2 * (2 * half + par + 1))
                pe.wait_ge(k_placed[par], 16 * PAIRS * (half + 1))

            def transpose_probs(n, b, first):
                pe.wait_ge(s["exp_done"], n + 1)
                if not (first and b == 0):
                    pe.wait_ge(s["probsT_copied"], n)
                for j in range(4):
                    last = nc.tensor.transpose(pt_bank[:, j * P:(j + 1) * P],
                                               probs[b % 4][:, 2 * j:2 * j + 2, :].rearrange("p a k -> p (a k)"), ident[:, :])
                last.then_inc(s["probsT_done"], 1)

            def heads(n, b, par, quad):
                pe.wait_ge(s["probsT_copied"], n + 1)
                q, into = b % 4, o_bank[b // 4]
                if q == 0:
                    wait_later(pe, s["o_scaled"], quad - 1)
                    wait_later(pe, s["recipT_copied"], quad)
                for j in range(4):
                    mm(into[32 * j:32 * (j + 1), q * P:(q + 1) * P], v_blk[par][:, b, j, :, :].rearrange("k a c -> k (a c)"),
                       pT[b % 2][:, j * P:(j + 1) * P], start=True, stop=True)
                pe.wait_ge(s["recip_done"], n + 1)
                nc.tensor.transpose(r_bank[:, q * P:(q + 1) * P], recip_rows[b % 2][:, :, :, :].rearrange("p a h c -> p (a h c)"),
                                    ident[:, :]).then_inc(s["heads_done"], 1)

            pe.wait_ge(s["consts_made"], 5)
            task_cT(0, 0, 1)
            pe.wait_ge(s["wk_loaded"], 16)
            task_k(0)
            task_xT(0, 0)
            pe.wait_ge(s["w_loaded"], 16 * 3)
            task_q(0)
            pe.wait_ge(s["ones_made"], 2)
            pe.wait_ge(s["mask_placed"], 48)
            group_placed(0, 0)
            for n in range(AHEAD):
                scores(n, n, 0)
            task_v(0)
            pe.wait_ge(s["small_loaded"], 16 * 4)
            mm(misc_b[:, 0:D], cols[:, 2:3].to_broadcast([P, P]), wo_s, start=True, stop=True).then_inc(s["attn_done"], 1)
            scores(AHEAD, AHEAD, 0)
            pe.wait_ge(s["gate_loaded"], 16)

            def body(g, half, par, first, last):
                nh, np_ = (half, 1) if par == 0 else (half + 1, 0)
                for b in range(BG):
                    n = BG * g + b
                    if b < BG - AHEAD - 1:
                        scores(n + AHEAD + 1, b + AHEAD + 1, par)
                    elif not last:
                        if b == BG - AHEAD - 1:
                            group_placed(nh, np_)
                        scores(n + AHEAD + 1, b + AHEAD + 1 - BG, np_)
                    transpose_probs(n, b, first)
                    if b == 0:
                        if not first:
                            heads(n - 1, BG - 1, 1 - par, None)
                    else:
                        heads(n - 1, b - 1, par, 2 * g + (b - 1) // 4)
                    at = LAST if last else MIDDLE
                    late = not (isinstance(g, int) and g < 2)
                    if b == at["logits"] and late:
                        task_logits(g - 2)
                    if not last:
                        if b == at["cT"]:
                            pe.wait_ge(s["v_copied"], 2 * (g + 1))
                            wait_later(pe, s["x2T_copied"], g - 1)
                            task_cT(g + 1, 1 - par, nh + 1)
                        if b == at["xT"]:
                            if first:
                                pe.wait_ge(s["out_bias_done"], 2)
                            wait_later(pe, s["route_step"], ROUTE_STEPS * (g - 2) + 1)
                            task_xT(g + 1, 1 - par)
                        if b == at["k"]:
                            task_k(g + 1)
                        if b == at["q"]:
                            task_q(g + 1)
                        if b == at["v"]:
                            task_v(g + 1)
                    if b == at["ranks"] and late:
                        if not last:
                            pe.wait_ge(s["xT_copied"], g + 2)
                        task_ranks(g - 2)
                    if b == at["attn"] and not first:
                        if not last:
                            pe.wait_ge(s["xT_copied"], g + 2)
                        wait_later(pe, s["place_step"], PLACE_STEPS * (g - 2) + 2)
                        task_attn(g - 1, 1 - par)
                    if b == at["x2T"] and not first:
                        pe.wait_ge(s["v_copied"], 2 * (g + 1) if last else 2 * (g + 2))
                        task_x2T(g - 1, 1 - par)

            groups(pe, body)
            g = GROUPS - 1

            def attn_half(h, into):
                pe.wait_ge(s["o_joined"], 2 * g + h + 1)
                for t in range(2):
                    last_mm = mm(into[:, t * D:(t + 1) * D], oT[1][:, (2 * h + t) * P:(2 * h + t + 1) * P], wo_s, start=True, stop=True)
                last_mm.then_inc(s["attn_done"], 1)

            pe.wait_ge(s["shifted"], BG * GROUPS)
            attn_half(0, score_bank[1])
            heads(BG * GROUPS - 1, BG - 1, 1, None)
            task_logits(g - 1)
            attn_half(1, o_bank[0])
            task_ranks(g - 1, score_bank[0])
            pe.wait_ge(s["o_scaled"], 2 * GROUPS)
            for h, half_bank in enumerate((misc_a, o_bank[1])):
                for t in range(2):
                    pe.wait_ge(s["tile_normalised"], 2 * h + t + 1)
                    last_mm = nc.tensor.transpose(half_bank[:, t * P:(t + 1) * P], row[1][:, 2 * h + t, 0:D], ident[:, :])
                last_mm.then_inc(s["x2T_half"], 1)
            pe.wait_ge(s["route_step"], ROUTE_STEPS * (g - 1) + 1)
            for h in range(2):
                pe.wait_ge(s["x2T_half_copied"], h + 1)
                last_mm = logits_of(range(2 * h, 2 * h + 2))
            last_mm.then_inc(s["logits_done"], 1)
            task_ranks(g)

            def slots_T(e, half, par, i):
                if isinstance(e, int) and e == 0 and i < 2:
                    pe.wait_ge(piece_loaded[i], 16)
                else:
                    pe.wait_ge(xs_loaded[par], 16 * (half + 1))
                wait_later(pe, s["xsT_split"], 3 * e + (1 if i == 2 else 0))
                for j in range(4 * i, min(4 * i + 4, J)):
                    last = nc.tensor.transpose(bank[4 + i % 2][:, (j - 4 * i) * P:(j - 4 * i + 1) * P], xs[par][:, j, 0:D], ident[:, :])
                last.then_inc(s["xsT_done"], 1)

            def up(e, par, i):
                a, b = 512 * i, min(512 * (i + 1), CAP)
                if i == 0:
                    pe.wait_ge(s["fc_split"], e + 1)
                pe.wait_ge(s["xsT_split"], 3 * e + i + 1)
                for c in range(HC):
                    wait_later(pe, s["gelu_done"], 3 * HC * e + HC * (i - 1) + c + 1)
                    for k, (w, t) in enumerate(((0, 0), (0, 1), (1, 0))):
                        last = mm(bank[c][:, 0:b - a], fc_r[par][w][:, c * P:(c + 1) * P], xsT[par][t][:, a:b], start=k == 0, stop=k == 2)
                    last.then_inc(s["up_done"], 1)

            def down_banks(e, k, last):
                if not last and k == 2:
                    pe.wait_ge(s["y_step"], 3 * e + 1)
                elif k == 0:
                    wait_later(pe, s["y_step"], 3 * e)
                elif k >= 4:
                    pe.wait_ge(s["gelu_done"], 3 * HC * (e + 1))

            def down(e, par, k, last):
                tiles, in_bank = (LAST_PARTS if last else PARTS)[k]
                pe.wait_ge(s["gelu_done"], 3 * HC * e + HC * (tiles[-1] // 4 + 1))
                down_banks(e, k, last)
                for j in tiles:
                    d = (j - tiles[0]) * D
                    for c in range(HC):
                        last_mm = mm(bank[in_bank][:, d:d + D], hT[:, c, j * P:(j + 1) * P], pj_s[par][:, c, :],
                                     start=c == 0, stop=c == HC - 1)
                    last_mm.then_inc(s["down_done"], 1)

            def nothing(into, done, count):
                for k in range(count):
                    mm(into[:, 0:8], all_ones[:, :], all_ones[:, 0:8], start=True, stop=True).then_inc(done, 1)

            def up_rest(e, par):
                with pe.If((long_experts >> e) & 1):
                    up(e, par, 2)
                with pe.Else():
                    pe.wait_ge(s["gelu_done"], 3 * HC * e + 2 * HC)
                    nothing(bank[HC - 1], s["up_done"], HC)

            def down_rest(e, par, last):
                k = len(LAST_PARTS if last else PARTS) - 1
                with pe.If((long_experts >> e) & 1):
                    down(e, par, k, last)
                with pe.Else():
                    pe.wait_ge(s["gelu_done"], 3 * HC * (e + 1))
                    down_banks(e, k, last)
                    nothing(bank[(LAST_PARTS if last else PARTS)[k][1]], s["down_done"], J - SURE)

            def expert(e, half, par, last):
                nh = half if par == 0 else half + 1
                up(e, par, 0)
                up(e, par, 1)
                if not last:
                    slots_T(e + 1, nh, 1 - par, 0)
                    slots_T(e + 1, nh, 1 - par, 1)
                up_rest(e, par)
                pe.wait_ge(pj_loaded[par], 16 * (half + 1))
                for k in range(len(LAST_PARTS if last else PARTS) - 1):
                    down(e, par, k, last)
                    if k == 0 and not last:
                        slots_T(e + 1, nh, 1 - par, 2)
                down_rest(e, par, last)

            for i in range(3):
                slots_T(0, 0, 0, i)
            pe.wait_ge(s["long_done"], 1)
            long_experts = pe.value_load(long_i[0:1, 0:1], min_val=0, max_val=2 ** E - 1)
            experts(pe, expert)


_INS = ["x", "ctx_1024", "mask_BxS2_ff1", "L0_xattn_Wq", "L0_xattn_bq", "L0_xattn_Wk", "L0_xattn_bk", "L0_xattn_Wv",
        "L0_xattn_bv", "L0_xattn_Wo", "L0_xattn_bo", "L0_ffn_gate_w", "L0_ffn_c_fc", "L0_ffn_fc_bias",
        "L0_ffn_c_proj", "L0_ffn_proj_bias"]


def kernel(**inputs):
    import concourse.bacc as bacc
    from concourse.bass_utils import run_bass_kernel_spmd

    nc = bacc.Bacc("TRN2", target_bir_lowering=False, num_devices=1)
    arrays, args = {}, []
    for name in _INS:
        a = np.ascontiguousarray(inputs[name])
        if name == "L0_ffn_fc_bias":
            e, _, h = a.shape
            a = np.ascontiguousarray(a.reshape(e * (h // P), P).T)
        arrays[f"in_{name}"] = a
        args.append(nc.dram_tensor(f"in_{name}", a.shape, mybir.dt.from_np(a.dtype), kind="ExternalInput").ap())
    shape = inputs["x"].shape
    args.append(nc.dram_tensor("out_x", shape, F32, kind="ExternalOutput").ap())
    xattn_moe(nc, *args)
    r = run_bass_kernel_spmd(nc, [arrays], core_ids=[0])
    return r.results[0]["out_x"]
```
